# Optimizing a Trainium2 kernel written in Bass

```python
import numpy as np
import jax
import jax.numpy as jnp

def _softmax(x, axis=-1):
    return jax.nn.softmax(x, axis=axis)

def _gelu(x):
    return jax.nn.gelu(x, approximate=True)

def _silu(x):
    return jax.nn.silu(x)

def _sigmoid(x):
    return jax.nn.sigmoid(x)

def _layernorm(x, axis=-1, eps=1e-05):
    m = jnp.mean(x, axis=axis, keepdims=True)
    v = jnp.var(x, axis=axis, keepdims=True)
    return (x - m) / jnp.sqrt(v + eps)

def _scatter_add(tgt, idx, src, axis=0):
    return tgt.at[idx].add(src)

def _segment_sum(src, seg, n):
    return jax.ops.segment_sum(src, seg, n)
kernel_name = 'mk_decoder_postln_d2_seqx_r4_e005d3'

def setup_inputs(seed: int=0):
    np.random.seed(seed)
    _w = jnp.asarray

    def _rec_inputs():
        import jax
        import jax.numpy as jnp
        _rk = jax.random.key(seed)
        x = 7.22e-05 + 1 * jax.random.normal(jax.random.fold_in(_rk, 1), (16, 112, 256), jnp.float32)
        _lenS = 112 - jax.random.randint(jax.random.fold_in(_rk, 7), (16,), 0, max(1, 112 // 4) + 1, jnp.int32)
        _lenS2 = 375 - jax.random.randint(jax.random.fold_in(_rk, 8), (16,), 0, max(1, 375 // 4) + 1, jnp.int32)
        _ctx_768P = jax.random.normal(jax.random.fold_in(_rk, 11), (16, 16, 192), jnp.float32)
        _ctx_768c = jax.random.dirichlet(jax.random.fold_in(_rk, 511), 0.3 * jnp.ones((16,), jnp.float32), (16, 375))
        _ctx_768t = jnp.einsum('bsk,bkd->bsd', _ctx_768c, _ctx_768P)
        _ctx_768t = _ctx_768t * jax.lax.rsqrt(jnp.mean(jnp.square(_ctx_768t)) + 1e-12) * 0.953939
        ctx_768 = 2.09791e-05 + 1.00001 * (_ctx_768t + 0.3 * jax.random.normal(jax.random.fold_in(_rk, 611), (16, 375, 192), jnp.float32))
        _validS = jnp.arange(112)[None, :] < _lenS[:, None]
        _validS2 = jnp.arange(375)[None, :] < _lenS2[:, None]
        _causal = jnp.tril(jnp.ones((112, 112), dtype=bool))
        mask_BxS_bf1 = jnp.ones((16, 112), dtype=bool)
        mask_BxS2_bf1 = jnp.ones((16, 375), dtype=bool)
        return (x, ctx_768, mask_BxS_bf1, mask_BxS2_bf1)
    x, ctx_768, mask_BxS_bf1, mask_BxS2_bf1 = _rec_inputs()

    def _L0_attn_setup():
        import jax, jax.numpy as jnp
        import numpy as np
        B_SZ, L, D_MODEL, D_STATE, D_OUT = (4, 512, 256, 16, 256)
        key = jax.random.key(seed)
        ks = jax.random.split(key, 8)
        x = jax.random.normal(ks[0], (B_SZ, L, D_MODEL), dtype=jnp.float32)
        A_log = jnp.tile(jnp.log(jnp.arange(1, D_STATE + 1, dtype=jnp.float32))[None, :], (D_MODEL, 1))
        W_dt = jax.random.normal(ks[1], (D_MODEL, 1), dtype=jnp.float32)
        b_dt = jax.random.normal(ks[2], (D_MODEL,), dtype=jnp.float32) * 0.02
        W_xp = jax.random.normal(ks[3], (2 * D_STATE, D_MODEL), dtype=jnp.float32) * D_MODEL ** (-0.5)
        b_xp = jax.random.normal(ks[4], (2 * D_STATE,), dtype=jnp.float32) * 0.02
        W_out = jax.random.normal(ks[5], (D_OUT, D_MODEL), dtype=jnp.float32) * D_MODEL ** (-0.5)
        b_out = jax.random.normal(ks[6], (D_OUT,), dtype=jnp.float32) * 0.02
        return {'x': x, 'A_log': A_log, 'W_dt': W_dt, 'b_dt': b_dt, 'W_xp': W_xp, 'b_xp': b_xp, 'W_out': W_out, 'b_out': b_out}
    _L0_attn_all = _L0_attn_setup()
    _L0_attn_in = {k: v for k, v in _L0_attn_all.items() if k in ('A_log', 'W_dt', 'b_dt', 'W_xp', 'b_xp', 'W_out', 'b_out')}
    del _L0_attn_all

    def _L0_xattn_setup():
        import jax, jax.numpy as jnp
        import numpy as np
        IN_DIM = 256
        CTX_DIM = 192
        NUM_HEADS = 16
        HEAD_DIM = IN_DIM // NUM_HEADS
        SCALE = 1.0 / float(np.sqrt(HEAD_DIM))
        key = jax.random.key(seed)
        ks = jax.random.split(key, 10)
        B, NQ, NKV = (8, 256, 128)
        s_in = 1.0 / float(np.sqrt(IN_DIM))
        s_ctx = 1.0 / float(np.sqrt(CTX_DIM))
        return {'x': jax.random.normal(ks[0], (B, NQ, IN_DIM), dtype=jnp.float32), 'context': jax.random.normal(ks[1], (B, NKV, CTX_DIM), dtype=jnp.float32), 'Wq': jax.random.normal(ks[2], (IN_DIM, IN_DIM), dtype=jnp.float32) * s_in, 'bq': jax.random.normal(ks[3], (IN_DIM,), dtype=jnp.float32) * 0.01, 'Wk': jax.random.normal(ks[4], (IN_DIM, CTX_DIM), dtype=jnp.float32) * s_ctx, 'bk': jax.random.normal(ks[5], (IN_DIM,), dtype=jnp.float32) * 0.01, 'Wv': jax.random.normal(ks[6], (IN_DIM, CTX_DIM), dtype=jnp.float32) * s_ctx, 'bv': jax.random.normal(ks[7], (IN_DIM,), dtype=jnp.float32) * 0.01, 'Wo': jax.random.normal(ks[8], (IN_DIM, IN_DIM), dtype=jnp.float32) * s_in, 'bo': jax.random.normal(ks[9], (IN_DIM,), dtype=jnp.float32) * 0.01}
    _L0_xattn_all = _L0_xattn_setup()
    _L0_xattn_in = {k: v for k, v in _L0_xattn_all.items() if k in ('Wq', 'bq', 'Wk', 'bk', 'Wv', 'bv', 'Wo', 'bo')}
    del _L0_xattn_all

    def _L0_ffn_setup():
        import jax, jax.numpy as jnp
        import numpy as np
        D_MODEL = 256
        N_EXPERTS = 8
        TOP_K = 2
        key = jax.random.key(seed)
        ks = jax.random.split(key, 8)
        d, e = (D_MODEL, N_EXPERTS)
        s = 1.0 / np.sqrt(d)
        return {'x': jax.random.normal(ks[0], (4, 512, d), dtype=jnp.float32), 'W_gate': jax.random.uniform(ks[1], (d, e), jnp.float32, -s, s), 'b_gate': jax.random.uniform(ks[2], (e,), jnp.float32, -s, s), 'W1': jax.random.uniform(ks[3], (e, d, d), jnp.float32, -s, s), 'b1': jax.random.uniform(ks[4], (e, d), jnp.float32, -s, s), 'W2': jax.random.uniform(ks[5], (e, d, d), jnp.float32, -s, s), 'b2': jax.random.uniform(ks[6], (e, d), jnp.float32, -s, s)}
    _L0_ffn_all = _L0_ffn_setup()
    _L0_ffn_in = {k: v for k, v in _L0_ffn_all.items() if k in ('W_gate', 'b_gate', 'W1', 'b1', 'W2', 'b2')}
    del _L0_ffn_all

    def _L1_attn_setup():
        import jax, jax.numpy as jnp
        import numpy as np
        L_LAYERS = 4
        D_MODEL = 256
        N_HEAD = 16
        D_FF = 1024
        SEQ = 256
        BATCH = 4
        WINDOW = 5 if False else 64
        EPS = 1e-05

        def _layernorm(x, g, b):
            mu = jnp.mean(x, axis=-1, keepdims=True)
            var = jnp.mean(jnp.square(x - mu), axis=-1, keepdims=True)
            return (x - mu) * jax.lax.rsqrt(var + EPS) * g + b

        def _make_mask(S, w):
            i = jnp.arange(S)[:, None]
            j = jnp.arange(S)[None, :]
            allowed = (j <= i) | (jnp.abs(i - j) <= w)
            return jnp.where(allowed, 0.0, -jnp.inf).astype(jnp.float32)
        key = jax.random.key(seed)
        ks = jax.random.split(key, 8)
        s = 0.02
        d, dff, L = (D_MODEL, D_FF, L_LAYERS)
        return {'x': jax.random.normal(ks[0], (SEQ, BATCH, d), jnp.float32), 'Wqkv': jax.random.normal(ks[1], (L, 3 * d, d), jnp.float32) * s, 'bqkv': jnp.zeros((L, 3 * d), jnp.float32), 'Wo': jax.random.normal(ks[2], (L, d, d), jnp.float32) * s, 'bo': jnp.zeros((L, d), jnp.float32), 'W1': jax.random.normal(ks[3], (L, dff, d), jnp.float32) * s, 'b1': jnp.zeros((L, dff), jnp.float32), 'W2': jax.random.normal(ks[4], (L, d, dff), jnp.float32) * s, 'b2': jnp.zeros((L, d), jnp.float32), 'g1': jnp.ones((L, d), jnp.float32), 'be1': jnp.zeros((L, d), jnp.float32), 'g2': jnp.ones((L, d), jnp.float32), 'be2': jnp.zeros((L, d), jnp.float32)}
    _L1_attn_all = _L1_attn_setup()
    _L1_attn_in = {k: v for k, v in _L1_attn_all.items() if k in ('Wqkv', 'bqkv', 'Wo', 'bo', 'W1', 'b1', 'W2', 'b2', 'g1', 'be1', 'g2', 'be2')}
    del _L1_attn_all

    def _L1_xattn_setup():
        import jax, jax.numpy as jnp
        import numpy as np
        B, T, DT, G, DV = (16, 128, 256, 144, 192)
        H, DH = (4, 32)
        INNER = H * DH
        HID = 4 * DT
        N_STATE = 64
        K_TOP = 32

        def layernorm(x, g, b, eps=1e-05):
            m = x.mean(-1, keepdims=True)
            v = x.var(-1, keepdims=True)
            return (x - m) * jax.lax.rsqrt(v + eps) * g + b

        def s4d(x, log_dt, A_re, A_im, C_re, C_im, D_skip):
            Bb, L, D = x.shape
            dt = jnp.exp(log_dt)
            A = A_re + 1j * A_im
            C = C_re + 1j * C_im
            dtA = dt[:, None] * A
            dC = C * (jnp.exp(dtA) - 1.0) / A
            powers = jnp.exp(dtA[:, :, None] * jnp.arange(L))
            K = 2.0 * jnp.einsum('dn,dnl->dl', dC, powers).real
            n = 2 * L
            Kf = jnp.fft.rfft(K, n=n, axis=-1)
            xf = jnp.fft.rfft(x, n=n, axis=1)
            y = jnp.fft.irfft(xf * Kf.T[None], n=n, axis=1)[:, :L]
            return y + x * D_skip
        key = jax.random.key(seed)
        ks = jax.random.split(key, 16)
        s = 0.02
        inp = {'x_text': jax.random.normal(ks[0], (B, T, DT), jnp.float32), 'x_vision': jax.random.normal(ks[1], (B, G, DV), jnp.float32), 'text_mask': jnp.ones((B, T), bool), 'vision_mask': jnp.ones((B, G), bool), 'Wq': jax.random.normal(ks[2], (DT, INNER), jnp.float32) * s, 'Wk': jax.random.normal(ks[3], (DV, INNER), jnp.float32) * s, 'Wv': jax.random.normal(ks[4], (DV, DT), jnp.float32) * s, 'W_film_in': jax.random.normal(ks[5], (DT, 2 * DT), jnp.float32) * s, 'b_film_in': jnp.zeros((2 * DT,), jnp.float32), 'W_film_out': jax.random.normal(ks[6], (DT, 2 * DT), jnp.float32) * s, 'b_film_out': jnp.zeros((2 * DT,), jnp.float32), 'g_norm_in': jnp.ones((DT,), jnp.float32), 'b_norm_in': jnp.zeros((DT,), jnp.float32), 'g_norm_out': jnp.ones((DT,), jnp.float32), 'b_norm_out': jnp.zeros((DT,), jnp.float32), 'g_ffn': jnp.ones((DT,), jnp.float32), 'b_ffn': jnp.zeros((DT,), jnp.float32), 'W1': jax.random.normal(ks[7], (DT, HID), jnp.float32) * s, 'b1': jnp.zeros((HID,), jnp.float32), 'W2': jax.random.normal(ks[8], (HID, DT), jnp.float32) * s, 'b2': jnp.zeros((DT,), jnp.float32), 'log_dt': jnp.log(0.001) + jax.random.uniform(ks[9], (DT,), jnp.float32) * (jnp.log(0.1) - jnp.log(0.001)), 'A_re': -0.5 * jnp.ones((DT, N_STATE), jnp.float32), 'A_im': jnp.tile(jnp.pi * jnp.arange(N_STATE, dtype=jnp.float32), (DT, 1)), 'C_re': jax.random.normal(ks[10], (DT, N_STATE), jnp.float32) * 0.5 ** 0.5, 'C_im': jax.random.normal(ks[11], (DT, N_STATE), jnp.float32) * 0.5 ** 0.5, 'D_skip': jax.random.normal(ks[12], (DT,), jnp.float32), 'mod_gate': jnp.array(0.5, jnp.float32)}
        return inp
    _L1_xattn_all = _L1_xattn_setup()
    _L1_xattn_in = {k: v for k, v in _L1_xattn_all.items() if k in ('Wq', 'Wk', 'Wv', 'W_film_in', 'b_film_in', 'W_film_out', 'b_film_out', 'g_norm_in', 'b_norm_in', 'g_norm_out', 'b_norm_out', 'g_ffn', 'b_ffn', 'W1', 'b1', 'W2', 'b2', 'log_dt', 'A_re', 'A_im', 'C_re', 'C_im', 'D_skip', 'mod_gate')}
    del _L1_xattn_all

    def _L1_ffn_setup():
        import jax, jax.numpy as jnp
        import numpy as np
        B, S, DIM = (4, 1024, 256)
        BASE_COUPLING = 0.1
        NUM_CYCLES = 3

        def _gelu(x):
            return jax.nn.gelu(x, approximate=False)

        def _coupling_net(h, w1, b1, w2, b2, w3, b3, w4, b4):
            h = _gelu(h @ w1 + b1)
            h = _gelu(h @ w2 + b2)
            h = _gelu(h @ w3 + b3)
            return jax.nn.sigmoid(h @ w4 + b4)

        def _global_net(h, w1, b1, w2, b2, w3, b3):
            h = _gelu(h @ w1 + b1)
            h = _gelu(h @ w2 + b2)
            return jax.nn.sigmoid(h @ w3 + b3)

        def _twist(x):
            o_r, o_i, p_r, p_i = jnp.split(x, 4, axis=-1)
            return jnp.concatenate([p_r, -p_i, -o_r, o_i], axis=-1)
        key = jax.random.key(seed)
        ks = jax.random.split(key, 9)
        d = DIM

        def w(k, fan_in, fan_out):
            return jax.random.normal(k, (fan_in, fan_out), dtype=jnp.float32) / np.sqrt(fan_in).astype(np.float32)
        inp = {'x': jax.random.normal(ks[0], (B, S, d), dtype=jnp.float32)}
        cn_dims = [(d, d), (d, d // 2), (d // 2, d // 4), (d // 4, 1)]
        for i, (a, b) in enumerate(cn_dims):
            inp[f'cn_w{i + 1}'] = w(ks[1 + i], a, b)
            inp[f'cn_b{i + 1}'] = jnp.zeros((b,), dtype=jnp.float32)
        gc_dims = [(d, d // 2), (d // 2, d // 4), (d // 4, 1)]
        for i, (a, b) in enumerate(gc_dims):
            inp[f'gc_w{i + 1}'] = w(ks[5 + i], a, b)
            inp[f'gc_b{i + 1}'] = jnp.zeros((b,), dtype=jnp.float32)
        inp['adaptive_range'] = jnp.full((1,), 0.2, dtype=jnp.float32)
        return inp
    _L1_ffn_all = _L1_ffn_setup()
    _L1_ffn_in = {k: v for k, v in _L1_ffn_all.items() if k in ('cn_w1', 'cn_b1', 'cn_w2', 'cn_b2', 'cn_w3', 'cn_b3', 'cn_w4', 'cn_b4', 'gc_w1', 'gc_b1', 'gc_w2', 'gc_b2', 'gc_w3', 'gc_b3', 'adaptive_range')}
    del _L1_ffn_all
    return {'x': x, 'ctx_768': ctx_768, 'mask_BxS_bf1': mask_BxS_bf1, 'mask_BxS2_bf1': mask_BxS2_bf1, 'L0_attn_A_log': _L0_attn_in['A_log'], 'L0_attn_W_dt': _L0_attn_in['W_dt'], 'L0_attn_b_dt': _L0_attn_in['b_dt'], 'L0_attn_W_xp': _L0_attn_in['W_xp'], 'L0_attn_b_xp': _L0_attn_in['b_xp'], 'L0_attn_W_out': _L0_attn_in['W_out'], 'L0_attn_b_out': _L0_attn_in['b_out'], 'L0_xattn_Wq': _L0_xattn_in['Wq'], 'L0_xattn_bq': _L0_xattn_in['bq'], 'L0_xattn_Wk': _L0_xattn_in['Wk'], 'L0_xattn_bk': _L0_xattn_in['bk'], 'L0_xattn_Wv': _L0_xattn_in['Wv'], 'L0_xattn_bv': _L0_xattn_in['bv'], 'L0_xattn_Wo': _L0_xattn_in['Wo'], 'L0_xattn_bo': _L0_xattn_in['bo'], 'L0_ffn_W_gate': _L0_ffn_in['W_gate'], 'L0_ffn_b_gate': _L0_ffn_in['b_gate'], 'L0_ffn_W1': _L0_ffn_in['W1'], 'L0_ffn_b1': _L0_ffn_in['b1'], 'L0_ffn_W2': _L0_ffn_in['W2'], 'L0_ffn_b2': _L0_ffn_in['b2'], 'L1_attn_Wqkv': _L1_attn_in['Wqkv'], 'L1_attn_bqkv': _L1_attn_in['bqkv'], 'L1_attn_Wo': _L1_attn_in['Wo'], 'L1_attn_bo': _L1_attn_in['bo'], 'L1_attn_W1': _L1_attn_in['W1'], 'L1_attn_b1': _L1_attn_in['b1'], 'L1_attn_W2': _L1_attn_in['W2'], 'L1_attn_b2': _L1_attn_in['b2'], 'L1_attn_g1': _L1_attn_in['g1'], 'L1_attn_be1': _L1_attn_in['be1'], 'L1_attn_g2': _L1_attn_in['g2'], 'L1_attn_be2': _L1_attn_in['be2'], 'L1_xattn_Wq': _L1_xattn_in['Wq'], 'L1_xattn_Wk': _L1_xattn_in['Wk'], 'L1_xattn_Wv': _L1_xattn_in['Wv'], 'L1_xattn_W_film_in': _L1_xattn_in['W_film_in'], 'L1_xattn_b_film_in': _L1_xattn_in['b_film_in'], 'L1_xattn_W_film_out': _L1_xattn_in['W_film_out'], 'L1_xattn_b_film_out': _L1_xattn_in['b_film_out'], 'L1_xattn_g_norm_in': _L1_xattn_in['g_norm_in'], 'L1_xattn_b_norm_in': _L1_xattn_in['b_norm_in'], 'L1_xattn_g_norm_out': _L1_xattn_in['g_norm_out'], 'L1_xattn_b_norm_out': _L1_xattn_in['b_norm_out'], 'L1_xattn_g_ffn': _L1_xattn_in['g_ffn'], 'L1_xattn_b_ffn': _L1_xattn_in['b_ffn'], 'L1_xattn_W1': _L1_xattn_in['W1'], 'L1_xattn_b1': _L1_xattn_in['b1'], 'L1_xattn_W2': _L1_xattn_in['W2'], 'L1_xattn_b2': _L1_xattn_in['b2'], 'L1_xattn_log_dt': _L1_xattn_in['log_dt'], 'L1_xattn_A_re': _L1_xattn_in['A_re'], 'L1_xattn_A_im': _L1_xattn_in['A_im'], 'L1_xattn_C_re': _L1_xattn_in['C_re'], 'L1_xattn_C_im': _L1_xattn_in['C_im'], 'L1_xattn_D_skip': _L1_xattn_in['D_skip'], 'L1_xattn_mod_gate': _L1_xattn_in['mod_gate'], 'L1_ffn_cn_w1': _L1_ffn_in['cn_w1'], 'L1_ffn_cn_b1': _L1_ffn_in['cn_b1'], 'L1_ffn_cn_w2': _L1_ffn_in['cn_w2'], 'L1_ffn_cn_b2': _L1_ffn_in['cn_b2'], 'L1_ffn_cn_w3': _L1_ffn_in['cn_w3'], 'L1_ffn_cn_b3': _L1_ffn_in['cn_b3'], 'L1_ffn_cn_w4': _L1_ffn_in['cn_w4'], 'L1_ffn_cn_b4': _L1_ffn_in['cn_b4'], 'L1_ffn_gc_w1': _L1_ffn_in['gc_w1'], 'L1_ffn_gc_b1': _L1_ffn_in['gc_b1'], 'L1_ffn_gc_w2': _L1_ffn_in['gc_w2'], 'L1_ffn_gc_b2': _L1_ffn_in['gc_b2'], 'L1_ffn_gc_w3': _L1_ffn_in['gc_w3'], 'L1_ffn_gc_b3': _L1_ffn_in['gc_b3'], 'L1_ffn_adaptive_range': _L1_ffn_in['adaptive_range']}

def reference(x, ctx_768, mask_BxS_bf1, mask_BxS2_bf1, L0_attn_A_log, L0_attn_W_dt, L0_attn_b_dt, L0_attn_W_xp, L0_attn_b_xp, L0_attn_W_out, L0_attn_b_out, L0_xattn_Wq, L0_xattn_bq, L0_xattn_Wk, L0_xattn_bk, L0_xattn_Wv, L0_xattn_bv, L0_xattn_Wo, L0_xattn_bo, L0_ffn_W_gate, L0_ffn_b_gate, L0_ffn_W1, L0_ffn_b1, L0_ffn_W2, L0_ffn_b2, L1_attn_Wqkv, L1_attn_bqkv, L1_attn_Wo, L1_attn_bo, L1_attn_W1, L1_attn_b1, L1_attn_W2, L1_attn_b2, L1_attn_g1, L1_attn_be1, L1_attn_g2, L1_attn_be2, L1_xattn_Wq, L1_xattn_Wk, L1_xattn_Wv, L1_xattn_W_film_in, L1_xattn_b_film_in, L1_xattn_W_film_out, L1_xattn_b_film_out, L1_xattn_g_norm_in, L1_xattn_b_norm_in, L1_xattn_g_norm_out, L1_xattn_b_norm_out, L1_xattn_g_ffn, L1_xattn_b_ffn, L1_xattn_W1, L1_xattn_b1, L1_xattn_W2, L1_xattn_b2, L1_xattn_log_dt, L1_xattn_A_re, L1_xattn_A_im, L1_xattn_C_re, L1_xattn_C_im, L1_xattn_D_skip, L1_xattn_mod_gate, L1_ffn_cn_w1, L1_ffn_cn_b1, L1_ffn_cn_w2, L1_ffn_cn_b2, L1_ffn_cn_w3, L1_ffn_cn_b3, L1_ffn_cn_w4, L1_ffn_cn_b4, L1_ffn_gc_w1, L1_ffn_gc_b1, L1_ffn_gc_w2, L1_ffn_gc_b2, L1_ffn_gc_w3, L1_ffn_gc_b3, L1_ffn_adaptive_range):
    import jax
    import jax.numpy as jnp

    def _L0_attn_ref(x, A_log, W_dt, b_dt, W_xp, b_xp, W_out, b_out):
        import jax, jax.numpy as jnp
        import numpy as np
        B_SZ, L, D_MODEL, D_STATE, D_OUT = (4, 512, 256, 16, 256)
        A = -jnp.exp(A_log)
        dt = jax.nn.softplus(x[:, :, 0:1] * W_dt[:, 0][None, None, :] + b_dt)
        BC = jnp.einsum('bld,ed->ble', x, W_xp) + b_xp
        Bm, Cm = (BC[..., :D_STATE], BC[..., D_STATE:])

        def step(state, inputs):
            dt_t, x_t, B_t, C_t = inputs
            dA = jnp.exp(A[None] * dt_t[:, :, None])
            dB = dt_t[:, :, None] * x_t[:, :, None] * B_t[:, None, :]
            state = dA * state + dB
            y = jnp.einsum('bdn,bn->bd', state, C_t)
            return (state, y)
        state0 = jnp.zeros((x.shape[0], D_MODEL, D_STATE), dtype=x.dtype)
        xs = (jnp.swapaxes(dt, 0, 1), jnp.swapaxes(x, 0, 1), jnp.swapaxes(Bm, 0, 1), jnp.swapaxes(Cm, 0, 1))
        _, ys = jax.lax.scan(step, state0, xs)
        y = jnp.swapaxes(ys, 0, 1)
        return jnp.einsum('bld,od->blo', y, W_out) + b_out

    def _L0_xattn_ref(x, context, Wq, bq, Wk, bk, Wv, bv, Wo, bo):
        import jax, jax.numpy as jnp
        import numpy as np
        IN_DIM = 256
        CTX_DIM = 192
        NUM_HEADS = 16
        HEAD_DIM = IN_DIM // NUM_HEADS
        SCALE = 1.0 / float(np.sqrt(HEAD_DIM))
        q = x @ Wq.T + bq
        k = context @ Wk.T + bk
        v = context @ Wv.T + bv
        B, NQ, _ = q.shape
        NKV = k.shape[1]
        q = q.reshape(B, NQ, NUM_HEADS, HEAD_DIM)
        k = k.reshape(B, NKV, NUM_HEADS, HEAD_DIM)
        v = v.reshape(B, NKV, NUM_HEADS, HEAD_DIM)
        attn = jnp.einsum('bihd,bjhd->bhij', q, k) * SCALE
        attn = jax.nn.softmax(attn, axis=-1)
        out = jnp.einsum('bhij,bjhd->bihd', attn, v)
        out = out.reshape(B, NQ, IN_DIM)
        return out @ Wo.T + bo

    def _L0_ffn_ref(x, W_gate, b_gate, W1, b1, W2, b2):
        import jax, jax.numpy as jnp
        import numpy as np
        D_MODEL = 256
        N_EXPERTS = 8
        TOP_K = 2
        B, T, d = x.shape
        xf = x.reshape(-1, d)
        scores = xf @ W_gate + b_gate
        topk_val, topk_idx = jax.lax.top_k(scores, TOP_K)
        onehot = jax.nn.one_hot(topk_idx, N_EXPERTS, dtype=xf.dtype)
        w = jnp.einsum('nk,nke->ne', topk_val, onehot)
        h = jax.nn.relu(jnp.einsum('nd,edh->neh', xf, W1) + b1)
        y = jnp.einsum('neh,ehd->ned', h, W2) + b2
        out = jnp.einsum('ned,ne->nd', y, w)
        return out.reshape(B, T, d)

    def _L1_attn_ref(x, Wqkv, bqkv, Wo, bo, W1, b1, W2, b2, g1, be1, g2, be2):
        import jax, jax.numpy as jnp
        import numpy as np
        L_LAYERS = 4
        D_MODEL = 256
        N_HEAD = 16
        D_FF = 1024
        SEQ = 256
        BATCH = 4
        WINDOW = 5 if False else 64
        EPS = 1e-05

        def _layernorm(x, g, b):
            mu = jnp.mean(x, axis=-1, keepdims=True)
            var = jnp.mean(jnp.square(x - mu), axis=-1, keepdims=True)
            return (x - mu) * jax.lax.rsqrt(var + EPS) * g + b

        def _make_mask(S, w):
            i = jnp.arange(S)[:, None]
            j = jnp.arange(S)[None, :]
            allowed = (j <= i) | (jnp.abs(i - j) <= w)
            return jnp.where(allowed, 0.0, -jnp.inf).astype(jnp.float32)
        S, B, d = x.shape
        h = N_HEAD
        hd = d // h
        mask = _make_mask(S, WINDOW)
        xb = jnp.transpose(x, (1, 0, 2))
        for l in range(Wqkv.shape[0]):
            qkv = jnp.einsum('bsd,ed->bse', xb, Wqkv[l]) + bqkv[l]
            q, k, v = jnp.split(qkv, 3, axis=-1)
            q = q.reshape(B, S, h, hd).transpose(0, 2, 1, 3)
            k = k.reshape(B, S, h, hd).transpose(0, 2, 1, 3)
            v = v.reshape(B, S, h, hd).transpose(0, 2, 1, 3)
            scores = jnp.einsum('bhqd,bhkd->bhqk', q, k) / jnp.sqrt(jnp.float32(hd))
            attn = jax.nn.softmax(scores + mask, axis=-1)
            o = jnp.einsum('bhqk,bhkd->bhqd', attn, v)
            o = o.transpose(0, 2, 1, 3).reshape(B, S, d)
            o = jnp.einsum('bsd,ed->bse', o, Wo[l]) + bo[l]
            xb = _layernorm(xb + o, g1[l], be1[l])
            ff = jax.nn.relu(jnp.einsum('bsd,fd->bsf', xb, W1[l]) + b1[l])
            ff = jnp.einsum('bsf,df->bsd', ff, W2[l]) + b2[l]
            xb = _layernorm(xb + ff, g2[l], be2[l])
        return jnp.transpose(xb, (1, 0, 2))

    def _L1_xattn_ref(x_text, x_vision, text_mask, vision_mask, Wq, Wk, Wv, W_film_in, b_film_in, W_film_out, b_film_out, g_norm_in, b_norm_in, g_norm_out, b_norm_out, g_ffn, b_ffn, W1, b1, W2, b2, log_dt, A_re, A_im, C_re, C_im, D_skip, mod_gate):
        import jax, jax.numpy as jnp
        import numpy as np
        B, T, DT, G, DV = (16, 128, 256, 144, 192)
        H, DH = (4, 32)
        INNER = H * DH
        HID = 4 * DT
        N_STATE = 64
        K_TOP = 32

        def layernorm(x, g, b, eps=1e-05):
            m = x.mean(-1, keepdims=True)
            v = x.var(-1, keepdims=True)
            return (x - m) * jax.lax.rsqrt(v + eps) * g + b

        def s4d(x, log_dt, A_re, A_im, C_re, C_im, D_skip):
            Bb, L, D = x.shape
            dt = jnp.exp(log_dt)
            A = A_re + 1j * A_im
            C = C_re + 1j * C_im
            dtA = dt[:, None] * A
            dC = C * (jnp.exp(dtA) - 1.0) / A
            powers = jnp.exp(dtA[:, :, None] * jnp.arange(L))
            K = 2.0 * jnp.einsum('dn,dnl->dl', dC, powers).real
            n = 2 * L
            Kf = jnp.fft.rfft(K, n=n, axis=-1)
            xf = jnp.fft.rfft(x, n=n, axis=1)
            y = jnp.fft.irfft(xf * Kf.T[None], n=n, axis=1)[:, :L]
            return y + x * D_skip
        Bb, Tt, D = x_text.shape
        Gg = x_vision.shape[1]
        Q = (x_text @ Wq).reshape(Bb, Tt, H, DH)
        K = (x_vision @ Wk).reshape(Bb, Gg, H, DH)
        scores = jnp.einsum('bthd,bghd->bhtg', Q, K) / np.sqrt(DH).astype(np.float32)
        scores = jnp.where(vision_mask[:, None, None, :], scores, -jnp.inf)
        topv, topi = jax.lax.top_k(scores, K_TOP)
        probs = jax.nn.softmax(topv, axis=-1)
        bi = jnp.arange(Bb)[:, None, None, None]
        hi = jnp.arange(H)[None, :, None, None]
        ti = jnp.arange(Tt)[None, None, :, None]
        attn = jnp.zeros_like(scores).at[bi, hi, ti, topi].set(probs)
        attn_mean = attn.mean(axis=1)
        V = x_vision @ Wv
        c_t = jnp.einsum('btg,bgd->btd', attn_mean, V)
        c_t = c_t * text_mask[..., None]
        x = layernorm(x_text, g_norm_in, b_norm_in)
        scale_in, shift_in = jnp.split(c_t @ W_film_in + b_film_in, 2, axis=-1)
        x = x * (1.0 + mod_gate * scale_in) + mod_gate * shift_in
        y = s4d(x, log_dt, A_re, A_im, C_re, C_im, D_skip)
        scale_out, shift_out = jnp.split(c_t @ W_film_out + b_film_out, 2, axis=-1)
        y = y * (1.0 + mod_gate * scale_out) + mod_gate * shift_out
        xt = x_text + y
        h = layernorm(xt, g_ffn, b_ffn)
        h = jax.nn.gelu(h @ W1 + b1, approximate=False) @ W2 + b2
        xt = xt + h
        return layernorm(xt, g_norm_out, b_norm_out)

    def _L1_ffn_ref(x, cn_w1, cn_b1, cn_w2, cn_b2, cn_w3, cn_b3, cn_w4, cn_b4, gc_w1, gc_b1, gc_w2, gc_b2, gc_w3, gc_b3, adaptive_range):
        import jax, jax.numpy as jnp
        import numpy as np
        B, S, DIM = (4, 1024, 256)
        BASE_COUPLING = 0.1
        NUM_CYCLES = 3

        def _gelu(x):
            return jax.nn.gelu(x, approximate=False)

        def _coupling_net(h, w1, b1, w2, b2, w3, b3, w4, b4):
            h = _gelu(h @ w1 + b1)
            h = _gelu(h @ w2 + b2)
            h = _gelu(h @ w3 + b3)
            return jax.nn.sigmoid(h @ w4 + b4)

        def _global_net(h, w1, b1, w2, b2, w3, b3):
            h = _gelu(h @ w1 + b1)
            h = _gelu(h @ w2 + b2)
            return jax.nn.sigmoid(h @ w3 + b3)

        def _twist(x):
            o_r, o_i, p_r, p_i = jnp.split(x, 4, axis=-1)
            return jnp.concatenate([p_r, -p_i, -o_r, o_i], axis=-1)
        global_context = x.mean(axis=1, keepdims=True)
        gf = _global_net(global_context, gc_w1, gc_b1, gc_w2, gc_b2, gc_w3, gc_b3)
        out = x
        for _ in range(NUM_CYCLES):
            tf = _coupling_net(out, cn_w1, cn_b1, cn_w2, cn_b2, cn_w3, cn_b3, cn_w4, cn_b4)
            combined = 0.7 * gf + 0.3 * tf
            coupling = BASE_COUPLING + adaptive_range * (combined - 0.5) * 2.0
            out = out + coupling * _twist(out)
        return out
    x = _layernorm(x + _L0_attn_ref(x, L0_attn_A_log, L0_attn_W_dt, L0_attn_b_dt, L0_attn_W_xp, L0_attn_b_xp, L0_attn_W_out, L0_attn_b_out), axis=-1)
    x = _layernorm(x + _L0_xattn_ref(x, ctx_768, L0_xattn_Wq, L0_xattn_bq, L0_xattn_Wk, L0_xattn_bk, L0_xattn_Wv, L0_xattn_bv, L0_xattn_Wo, L0_xattn_bo), axis=-1)
    x = _layernorm(x + _L0_ffn_ref(x, L0_ffn_W_gate, L0_ffn_b_gate, L0_ffn_W1, L0_ffn_b1, L0_ffn_W2, L0_ffn_b2), axis=-1)
    x = _layernorm(x + _L1_attn_ref(x, L1_attn_Wqkv, L1_attn_bqkv, L1_attn_Wo, L1_attn_bo, L1_attn_W1, L1_attn_b1, L1_attn_W2, L1_attn_b2, L1_attn_g1, L1_attn_be1, L1_attn_g2, L1_attn_be2), axis=-1)
    x = _layernorm(x + _L1_xattn_ref(x, ctx_768, mask_BxS_bf1, mask_BxS2_bf1, L1_xattn_Wq, L1_xattn_Wk, L1_xattn_Wv, L1_xattn_W_film_in, L1_xattn_b_film_in, L1_xattn_W_film_out, L1_xattn_b_film_out, L1_xattn_g_norm_in, L1_xattn_b_norm_in, L1_xattn_g_norm_out, L1_xattn_b_norm_out, L1_xattn_g_ffn, L1_xattn_b_ffn, L1_xattn_W1, L1_xattn_b1, L1_xattn_W2, L1_xattn_b2, L1_xattn_log_dt, L1_xattn_A_re, L1_xattn_A_im, L1_xattn_C_re, L1_xattn_C_im, L1_xattn_D_skip, L1_xattn_mod_gate), axis=-1)
    x = _layernorm(x + _L1_ffn_ref(x, L1_ffn_cn_w1, L1_ffn_cn_b1, L1_ffn_cn_w2, L1_ffn_cn_b2, L1_ffn_cn_w3, L1_ffn_cn_b3, L1_ffn_cn_w4, L1_ffn_cn_b4, L1_ffn_gc_w1, L1_ffn_gc_b1, L1_ffn_gc_w2, L1_ffn_gc_b2, L1_ffn_gc_w3, L1_ffn_gc_b3, L1_ffn_adaptive_range), axis=-1)
    return x

_drawn_inputs = setup_inputs


def setup_inputs(seed=0):
    import zlib

    import numpy as np

    out = dict(_drawn_inputs(seed))
    spreads = {'L1_attn_bqkv': (0.0, 0.1),
     'L1_attn_bo': (0.0, 0.1),
     'L1_attn_b1': (0.0, 0.1),
     'L1_attn_b2': (0.0, 0.1),
     'L1_attn_g1': (1.0, 0.2),
     'L1_attn_be1': (0.0, 0.1),
     'L1_attn_g2': (1.0, 0.2),
     'L1_attn_be2': (0.0, 0.1),
     'L1_xattn_b_film_in': (0.0, 0.1),
     'L1_xattn_b_film_out': (0.0, 0.271),
     'L1_xattn_g_norm_in': (1.0, 0.2),
     'L1_xattn_b_norm_in': (0.0, 0.1),
     'L1_xattn_g_norm_out': (1.0, 0.2),
     'L1_xattn_b_norm_out': (0.0, 0.1),
     'L1_xattn_g_ffn': (1.0, 0.6),
     'L1_xattn_b_ffn': (0.0, 0.8),
     'L1_xattn_b1': (0.0, 0.732),
     'L1_xattn_b2': (0.0, 0.1),
     'L1_xattn_A_re': (-0.5, 0.576),
     'L1_ffn_cn_b1': (0.0, 2.0),
     'L1_ffn_cn_b2': (0.0, 2.0),
     'L1_ffn_cn_b3': (0.0, 2.0),
     'L1_ffn_gc_b1': (0.0, 0.8),
     'L1_ffn_gc_b2': (0.0, 0.8)}
    factors = {'L0_attn_b_dt': 3.597,
     'L0_attn_b_out': 3.445,
     'L0_xattn_bq': 22.005,
     'L0_xattn_bk': 64.0,
     'L0_xattn_bv': 4.118,
     'L0_xattn_bo': 3.272,
     'L0_ffn_b1': 3.922,
     'L1_xattn_Wq': 7.419,
     'L1_xattn_Wk': 7.217,
     'L1_xattn_Wv': 2.883,
     'L1_xattn_W_film_in': 3.686,
     'L1_xattn_W_film_out': 4.503,
     'L1_ffn_cn_w1': 7.255,
     'L1_ffn_cn_w2': 8.0,
     'L1_ffn_cn_w3': 6.45,
     'L1_ffn_cn_w4': 6.421,
     'L1_ffn_gc_w1': 5.154,
     'L1_ffn_gc_w2': 4.933,
     'L1_ffn_gc_w3': 5.378}
    for name, (base, spread) in spreads.items():
        noise = np.random.default_rng([zlib.crc32(name.encode()), seed]).standard_normal(out[name].shape)
        drawn = base * np.exp(spread * noise) if base else spread * noise
        out[name] = jnp.asarray(drawn.astype(out[name].dtype))
    for name, factor in factors.items():
        out[name] = (out[name] * factor).astype(out[name].dtype)
    return out
```

```python
from contextlib import ExitStack

import concourse.bass as bass
from concourse import mybir

F32 = mybir.dt.float32
BF16 = mybir.dt.bfloat16
I32 = mybir.dt.int32
U8 = mybir.dt.uint8
ALU = mybir.AluOpType
ACT = mybir.ActivationFunctionType
AX = mybir.AxisListType

P = 128
B, T, D = 16, 112, 256
TOK = B * T
KC = D // P
S2, DC = 375, 192
CR = [P, DC - P]
JR, JC = 125, 3
NQ, QB = 4, 4
QT = QB * T
EPS = 1e-5
NS, KLOW = 64, 16
KHIGH = T // KLOW


def build(nc, dr, out):
    ctx = ExitStack()
    with ctx:
        def sem(name):
            return ctx.enter_context(nc.semaphore(name))

        def sb(name, shape, dt=F32, pool=None):
            return (pool or ctx).enter_context(nc.sbuf_tensor(name, shape, dt))

        XF = sb("XF", [P, KC, TOK])
        XD = sb("XD", [P, KC, TOK])
        XA = sb("XA", [P, B, D])
        ident = sb("ident", [P, P])
        cols = sb("cols", [P, COLS.size])
        rows = sb("rows", [P, ROWS.size])
        wa = sb("wa", [P, KC, 96 + D])
        ident16 = sb("ident16", [P, P], BF16)
        wb = sb("wb", [P, KC, 4 * D])
        ln_st = sb("ln_st", [P, 4, QB, 6])
        ln_mv = sb("ln_mv", [P, 4, QB, 2])
        ln_ve = sb("ln_ve", [P, 4, QB])
        ln_rs = sb("ln_rs", [P, 4, QB])
        halves = sb("halves", [P, QB])
        XG = XA[:, :, :].rearrange("p b d -> p (b d)")

        PS = ctx.enter_context(nc.psum_tensor("PS", [P, 8, 512], F32))
        ps = [PS[:, i, :] for i in range(8)]

        ssm = ExitStack()
        dt_f = sb("dt_f", [P, KC, TOK], pool=ssm)
        u_f = sb("u_f", [P, KC, TOK], pool=ssm)
        bc_parts = sb("bc_parts", [96, TOK], BF16, pool=ssm)
        bc_f = sb("bc_f", [96, QT], pool=ssm)
        bc_16 = sb("bc_16", [96, QT], BF16, pool=ssm)
        negA = sb("negA", [P, KC, 16], pool=ssm)
        dA = sb("dA", [P, 16, QB, T], pool=ssm)
        st_h = sb("st_h", [P, 2, 16, QT], pool=ssm)
        ssm.close()

        wc = sb("wc", [P, 2 * 8 * KC * D])
        ENC_W = 6656
        enc_w0 = sb("enc_w0", [P, ENC_W])
        xat = ExitStack()
        qm = sb("qm", [P, 2, KC, TOK], pool=xat)
        ctx_t = sb("ctx_t", [P, 2, 2, S2], pool=xat)
        k_t = sb("k_t", [P, 2, KC, S2], pool=xat)
        v_t = sb("v_t", [P, 2, JC, D], pool=xat)
        prob = sb("prob", [P, 3, S2], pool=xat)
        prob_t = sb("prob_t", [P, 2, JC, T], pool=xat)
        nmax = sb("nmax", [P, 4], pool=xat)
        sums = sb("sums", [P, 4], pool=xat)
        o_t = sb("o_t", [P, 2, 4, T], pool=xat)
        wo4 = enc_w0[:, 0:4 * D].rearrange("p (k n) -> p k n", k=4)
        bq_m = sb("bq_m", [P, 2, KC], pool=xat)
        kg = sb("kg", [P, 12, KC, NS], pool=xat)
        kg_low = sb("kg_low", [P, 2, KC, KLOW, NS], pool=xat)
        kg_high = sb("kg_high", [P, 2, KC, KHIGH, NS], pool=xat)
        k_pad = sb("k_pad", [P, KC, 2 * T], pool=xat)
        xat.close()
        E8 = 8
        moe = ExitStack()
        gate_s = sb("gate_s", [P, B, 16], pool=moe)
        gate_r = sb("gate_r", [P, B, 16], pool=moe)
        gate_m = sb("gate_m", [P, B, 8], pool=moe)
        gate_p = sb("gate_p", [P, B, 8], pool=moe)
        gate_w = sb("gate_w", [P, B, E8], pool=moe)
        gate_wt = sb("gate_wt", [E8, TOK], pool=moe)
        moe_small = sb("moe_small", [P, KC * E8], pool=moe)
        moe_b2 = sb("moe_b2", [E8, D], pool=moe)
        h_t = sb("h_t", [P, 2, KC, QT], pool=moe)
        moe.close()
        LAYERS, ROUNDS = 4, 7
        RT = TOK // ROUNDS
        ENC_ROWS = ("bv", "bo", "g1", "be1", "b2", "g2", "be2")
        enc = ExitStack()
        enc_rows = sb("enc_rows", [P, 2, len(ENC_ROWS), D], pool=enc)
        xg0 = sb("xg0", [P, 2 * ROUNDS, D], pool=enc)
        bq4 = sb("bq4", [P, LAYERS * KC], pool=enc)
        q_f = sb("q_f", [P, 2, KC, RT], pool=enc)
        k_f = sb("k_f", [P, 2, KC, RT], pool=enc)
        q_x = sb("q_x", [P, KC, 16, P], pool=enc)
        s_m = sb("s_m", [P, 32, 16], pool=enc)
        s_x = sb("s_x", [P, 32], pool=enc)
        s_s = sb("s_s", [P, 32], pool=enc)
        p_x = sb("p_x", [P, 4, 8, 8, 16], pool=enc)
        v_g = sb("v_g", [P, 2, 2, D], pool=enc)
        o_f = sb("o_f", [P, 2, 4, P], pool=enc)
        x1 = sb("x1", [P, 2, 2, D], pool=enc)
        x1f = sb("x1f", [P, 2, KC, RT], pool=enc)
        enc.close()
        h_ff = wb[:, :, :].rearrange("p k d -> p (k d)").rearrange("p (m n) -> p m n", m=8)
        XH = 4
        TD = 16
        s4x = ExitStack()
        s4a = ExitStack()
        t_ring = sb("t_ring", [T, 4, TD, T], pool=s4x)
        c_t = sb("c_t", [P, KC, TOK], pool=s4x)
        q_e = sb("q_e", [P, TOK], pool=s4a)
        ctx_f = sb("ctx_f", [P, 2, 2, S2], pool=s4a)
        ctx_k = sb("ctx_k", [JR, 2, JC, DC], pool=s4a)
        k_e = sb("k_e", [P, 2, S2], pool=s4a)
        w_s = sb("w_s", [T, 2, S2], pool=s4a)
        e_p = sb("e_p", [T, 2 * XH, S2], pool=s4a)
        top8 = sb("top8", [T, 2, 4, 8], pool=s4a)
        neg_m = sb("neg_m", [T, 4], pool=s4a)
        e_sum = sb("e_sum", [T, 2, XH], pool=s4a)
        e_rs = sb("e_rs", [T, 2, XH], pool=s4a)
        dg = sb("dg", [T, 2, XH, T], pool=s4a)
        at_t = sb("at_t", [JR, 2, JC, T], pool=s4a)
        msk8 = sb("msk8", [P, S2], U8, pool=s4a)
        mskb = sb("mskb", [P, S2], pool=s4a)
        tmk8 = sb("tmk8", [T, B], U8, pool=s4a)
        tmk = sb("tmk", [T, B], pool=s4a)
        s4a.close()
        s4b = ExitStack()
        x2 = sb("x2", [T, B, D], pool=s4b)
        film_t = sb("film_t", [T, 2, 2 * D], pool=s4b)
        hn = sb("hn", [T, QB, D], pool=s4b)
        hf = sb("hf", [P, KC, QT], pool=s4b)
        s4b.close()
        s4x.close()
        m1 = XD
        g_t = XD[:, :, :].rearrange("p k n -> p (k n)").rearrange("p (m n) -> p m n", m=8)
        ew = enc_w0[:, 0:3072]
        e_wq = ew[:, 0:256].rearrange("p (k n) -> p k n", k=2)
        e_wk = ew[:, 256:512].rearrange("p (k n) -> p k n", k=2)
        e_wv = ew[:, 512:1024].rearrange("p (k n) -> p k n", k=2)
        e_wf = ew[:, 1024:3072].rearrange("p (s k n) -> p s k n", s=2, k=2)
        e_rows = enc_w0[:, 3072:6144]
        e_w1 = wc[:, 0:2048].rearrange("p (k n) -> p k n", k=2)
        flip = wc[0:T, 5250:5250 + T]
        FLIPS = B // 2
        e_w2 = wc[:, 2048:4096].rearrange("p (k n) -> p k n", k=8)
        CYCLES, HB = 3, B // 2
        twi = ExitStack()
        y_a = sb("y_a", [T, B, D], pool=twi)
        y_b = sb("y_b", [T, B, D], pool=twi)
        n_h1 = sb("n_h1", [P, KC, QT], pool=twi)
        n_h2 = sb("n_h2", [P, QT], pool=twi)
        n_h3 = sb("n_h3", [P // 2, QT], pool=twi)
        x_sum = sb("x_sum", [P, KC, B], pool=twi)
        n_g1 = sb("n_g1", [P, B], pool=twi)
        n_g2 = sb("n_g2", [P // 2, B], pool=twi)
        cpl_0 = sb("cpl_0", [T, B], pool=twi)
        cpl_3 = sb("cpl_3", [T, 1], pool=twi)
        tf_s = sb("tf_s", [T, HB], pool=twi)
        cpl = sb("cpl", [T, 2, HB], pool=twi)
        twi.close()

        x_loaded, const_loaded, wa_loaded, wb_loaded = (
            sem("x_loaded"), sem("const_loaded"), sem("wa_loaded"), sem("wb_loaded"))
        dve_step, act_step, pool_step = sem("dve_step"), sem("act_step"), sem("pool_step")
        ln_var, ln_rstd = sem("ln_var"), sem("ln_rstd")
        res_biased = sem("res_biased")
        bc_ready, bc_copied = sem("bc_ready"), sem("bc_copied")
        z_ready, z_abs, z_pos, dt_log, dt_done = (
            sem("z_ready"), sem("z_abs"), sem("z_pos"), sem("dt_log"), sem("dt_done"))
        bc_split = sem("bc_split")
        scaled = sem("scaled")
        bcast_ready, bcast_used = sem("bcast_ready"), sem("bcast_used")
        pair_added = sem("pair_added")
        dA_ready, scan_done = sem("dA_ready"), sem("scan_done")
        y_ready, y_copied = sem("y_ready"), sem("y_copied")
        proj_ready, proj_added = sem("proj_ready"), sem("proj_added")
        norm_done, xt_ready, xf_ready = sem("norm_done"), sem("xt_ready"), sem("xf_ready")
        out_stored = sem("out_stored")

        class Chain:

            def __init__(self, eng, sem_):
                self.eng, self.sem, self.n = eng, sem_, 0

            def __call__(self, ins):
                self.n += 1
                ins.then_inc(self.sem, 1)
                self.eng.wait_ge(self.sem, self.n)

            def mark(self, ins):
                self.n += 1
                ins.then_inc(self.sem, 1)
                return self.n

            def after(self, n):
                self.eng.wait_ge(self.sem, n)

        def row(name, n=P):
            a, w = ROWS.at[name]
            return rows[0:n, a:a + w]

        def col(name, n=P, i=0):
            a, w = COLS.at[name]
            return cols[0:n, a + i:a + i + 1]

        jobs = {"dve": 0, "pool": 0}

        def norm_stats(dve, link, tiles, n=T):
            k = jobs["dve"]
            for i, t in enumerate(tiles):
                last = dve.bn_stats(ln_st[0:n, k % 4, i, :], t)
            link(last)
            for i, t in enumerate(tiles):
                last = dve.bn_aggr(ln_mv[0:n, k % 4, i, :], ln_st[0:n, k % 4, i, :])
            last.then_inc(ln_var, 1)
            jobs["dve"] = k + 1
            return k

        def norm_apply(dve, k, i, out_, in_, n=T):
            if i == 0:
                dve.wait_ge(ln_rstd, k + 1)
            return dve.tensor_scalar(out_, in_, ln_mv[0:n, k % 4, i, 0:1], ln_rs[0:n, k % 4, i:i + 1],
                                     ALU.subtract, ALU.mult)

        def norm_root(pool, link, g, n=T):
            k = jobs["pool"]
            pool.wait_ge(ln_var, k + 1)
            link(pool.tensor_scalar(ln_ve[0:n, k % 4, 0:g], ln_mv[0:n, k % 4, 0:g, 1], EPS, None, ALU.add))
            pool.tensor_tensor(ln_rs[0:n, k % 4, 0:g], ln_ve[0:n, k % 4, 0:g], halves[0:n, 0:g],
                               ALU.pow).then_inc(ln_rstd, 1)
            jobs["pool"] = k + 1

        UNITS = [(c, q) for c in range(KC) for q in range(NQ)]

        def ssm_load(sp):
            sp.dma_start(XF[:, :, :], dr["xT"].rearrange("c p n -> p c n")).then_inc(x_loaded, 16)
            sp.dma_start(wa[:, :, :], dr["wa"]).then_inc(wa_loaded, 16)
            sp.dma_start(cols[:, :], dr["cols"]).then_inc(const_loaded, 16)
            sp.dma_start(ident[:, :], dr["ident"]).then_inc(const_loaded, 16)
            sp.dma_start(rows[:, :], dr["rows"].partition_broadcast(P)).then_inc(const_loaded, 16)
            sp.dma_start(XA[0:T, :, :], dr["x"].rearrange("b t d -> t b d")).then_inc(x_loaded, 16)
            sp.dma_start(wb[:, :, :], dr["wb"]).then_inc(wb_loaded, 16)

        def transposed_to_features(pe, q, first_bank, norm_value):
            pe.wait_ge(norm_done, norm_value)
            for c in range(KC):
                for i in range(QB):
                    last = pe.transpose(ps[first_bank + c][:, i * T:(i + 1) * T],
                                        XA[0:T, q * QB + i, c * P:(c + 1) * P], ident[0:T, 0:T])
            last.then_inc(xt_ready, 1)

        def ssm_pe(pe):
            pe.wait_ge(x_loaded, 32)
            pe.wait_ge(wa_loaded, 16)
            pe.wait_ge(const_loaded, 48)
            for i, (c, q) in enumerate(UNITS):
                if i >= 2:
                    pe.wait_ge(z_pos, i - 1)
                pe.matmul(ps[4 + i % 2][:, 0:QT], row("w_dt", 1)[:, c * P:(c + 1) * P],
                          XF[0:1, 0, q * QT:(q + 1) * QT], start=True, stop=True).then_inc(z_ready, 1)
            for q in range(NQ):
                if q >= 2:
                    pe.wait_ge(bc_copied, q - 1)
                for k in range(KC):
                    last = pe.matmul(ps[6 + q % 2][0:96, 0:QT], wa[:, k, 0:96],
                                     XF[:, k, q * QT:(q + 1) * QT], start=(k == 0), stop=(k == KC - 1))
                last.then_inc(bc_ready, 1)
            pe.wait_ge(bc_split, NQ)

            def broadcast(i, half, pair):
                c, q = UNITS[i]
                j = i * 16 + half * 8 + pair
                if j >= 2:
                    pe.wait_ge(bcast_used, j - 1)
                for m in range(2):
                    s = half * 16 + 2 * pair + m
                    last = pe.matmul(ps[2 * (j % 2) + m][:, 0:QT], ident16[0:96, s:s + 1].to_broadcast([96, P]),
                                     bc_parts[0:96, q * QT:(q + 1) * QT], start=True, stop=True)
                last.then_inc(bcast_ready, 1)

            def sum_states(i, pair):
                pe.wait_ge(pair_added, i * 8 + pair + 1)
                if pair == 0 and i >= 2:
                    pe.wait_ge(y_copied, i - 1)
                last = pe.matmul(ps[4 + i % 2][:, 0:QT], ident[:, :], st_h[:, i % 2, 2 * pair, :],
                                 start=(pair == 0), stop=(pair == 7))
                if pair == 7:
                    last.then_inc(y_ready, 1)

            pe.wait_ge(z_pos, len(UNITS))
            for pair in range(2):
                broadcast(0, 0, pair)
            for i in range(len(UNITS)):
                for pair in range(2, 8):
                    broadcast(i, 0, pair)
                broadcast(i, 1, 0)
                broadcast(i, 1, 1)
                for pair in range(2, 8):
                    broadcast(i, 1, pair)
                    sum_states(i, pair - 2)
                if i + 1 < len(UNITS):
                    broadcast(i + 1, 0, 0)
                sum_states(i, 6)
                if i + 1 < len(UNITS):
                    broadcast(i + 1, 0, 1)
                sum_states(i, 7)
            pe.wait_ge(y_copied, len(UNITS))
            for q in range(NQ + 1):
                if q < NQ:
                    if q >= 2:
                        pe.wait_ge(proj_added, QB * (q - 1))
                    for i in range(QB):
                        b = q * QB + i
                        for k in range(KC):
                            last = pe.matmul(ps[4 + 2 * (q % 2) + i // 2][0:T, (i % 2) * D:(i % 2 + 1) * D],
                                             XD[:, k, b * T:(b + 1) * T], wa[:, k, 96:96 + D],
                                             start=(k == 0), stop=(k == KC - 1))
                    last.then_inc(proj_ready, 1)
                if q >= 1:
                    if q >= 3:
                        pe.wait_ge(xf_ready, 2 * (q - 2))
                    transposed_to_features(pe, q - 1, 2 * ((q - 1) % 2), q)

        def ssm_act(act):
            act.wait_ge(const_loaded, 48)
            for c in range(KC):
                act.activation(negA[:, c, :], cols[:, COLS.at["A_log"][0] + 16 * c:][:, 0:16], ACT.Exp)\
                   .then_inc(act_step, 1)
            for i, (c, q) in enumerate(UNITS):
                act.wait_ge(z_ready, i + 1)
                t = u_f[:, c, q * QT:(q + 1) * QT]
                act.activation(t, ps[4 + i % 2][:, 0:QT], ACT.Abs, bias=col("b_dt", i=c)).then_inc(z_abs, 1)
                act.wait_ge(z_abs, i + 1)
                act.activation(t, t, ACT.Exp, scale=-1.0).then_inc(act_step, 1)
            for q in range(NQ):
                act.wait_ge(bc_ready, q + 1)
                if q >= 1:
                    act.wait_ge(bc_split, q)
                act.activation(bc_f[:, :], ps[6 + q % 2][0:96, 0:QT], ACT.Identity,
                               bias=col("b_xp", 96)).then_inc(bc_copied, 1)
            for i, (c, q) in enumerate(UNITS):
                t = u_f[:, c, q * QT:(q + 1) * QT]
                act.wait_ge(act_step, KC + i + 1)
                act.activation(t, t, ACT.Ln, bias=1.0).then_inc(dt_log, 1)
            act.wait_ge(dt_done, len(UNITS))
            act.wait_ge(scaled, 1)
            for i, (c, q) in enumerate(UNITS):
                if i >= 1:
                    act.wait_ge(scan_done, i)
                for n in range(16):
                    last = act.activation(dA[:, n, :, :], dt_f[:, c, q * QT:(q + 1) * QT].rearrange(
                        "p (b t) -> p b t", t=T), ACT.Exp, scale=negA[:, c, n:n + 1])
                last.then_inc(dA_ready, 1)
                if i >= 1:
                    ssm_copy_y(act, i - 1)
            ssm_copy_y(act, len(UNITS) - 1)
            for q in range(NQ):
                copy_features(act, q, 2 * (q % 2), q + 1)

        def ssm_copy_y(act, i):
            c, q = UNITS[i]
            act.wait_ge(y_ready, i + 1)
            act.copy(XD[:, c, q * QT:(q + 1) * QT], ps[4 + i % 2][:, 0:QT]).then_inc(y_copied, 1)

        def copy_features(act, q, first_bank, value, dest=XF):
            act.wait_ge(xt_ready, value)
            for c in range(KC):
                src = ps[first_bank + c][:, 0:QT]
                if dest is XF:
                    dst = XF[:, c, q * QT:(q + 1) * QT]
                else:
                    dst = XD[:, c, :].rearrange("p (t b) -> p b t", b=B)[:, q * QB:(q + 1) * QB, :]
                    src = src.rearrange("p (b t) -> p b t", t=T)
                act.copy(dst, src).then_inc(xf_ready, 1)

        def ssm_dve(dve, link):
            dve.wait_ge(const_loaded, 48)
            for k in range(3):
                last = dve.tensor_copy(ident16[32 * k:32 * k + 32, 0:32], ident[32 * k:32 * k + 32,
                                                                                32 * k:32 * k + 32])
            link(last)
            dve.wait_ge(x_loaded, 32)
            dve.wait_ge(act_step, KC)
            dve.tensor_scalar(negA[:, :, :], negA[:, :, :], -1.0, None, ALU.mult).then_inc(scaled, 1)
            for i, (c, q) in enumerate(UNITS):
                dve.wait_ge(z_abs, i + 1)
                dve.tensor_scalar(dt_f[:, c, q * QT:(q + 1) * QT], ps[4 + i % 2][:, 0:QT],
                                  col("b_dt", i=c), 0.0, ALU.add, ALU.max).then_inc(z_pos, 1)
            for q in range(NQ):
                w = slice(q * QT, (q + 1) * QT)
                dve.wait_ge(bc_copied, q + 1)
                for part in range(3):
                    if part < 2:
                        link(dve.tensor_copy(bc_16[:, :], bc_f[:, :]))
                        n = slice(32 * part, 32 * part + 32)
                        dve.tensor_copy(bc_parts[n, w], bc_16[n, :])
                        link(dve.tensor_tensor(bc_f[:, :], bc_f[:, :], bc_16[:, :], ALU.subtract))
                    else:
                        dve.tensor_copy(bc_parts[64:96, w], bc_f[64:96, :]).then_inc(bc_split, 1)
            dve.wait_ge(z_pos, len(UNITS))
            for i, (c, q) in enumerate(UNITS):
                w = slice(q * QT, (q + 1) * QT)
                dve.wait_ge(dt_log, i + 1)
                dve.tensor_tensor(dt_f[:, c, w], dt_f[:, c, w], u_f[:, c, w], ALU.add).then_inc(dt_done, 1)
                dve.wait_ge(dt_done, i + 1)
                link(dve.tensor_tensor(u_f[:, c, w], dt_f[:, c, w], XF[:, c, w], ALU.mult))
            for i, (c, q) in enumerate(UNITS):
                h = st_h[:, i % 2, :, :]
                u2 = u_f[:, c:c + 1, q * QT:(q + 1) * QT].to_broadcast([P, 2, QT])
                if i >= 2:
                    dve.wait_ge(y_ready, i - 1)
                for half in range(2):
                    if half == 1:
                        dve.wait_ge(dA_ready, i + 1)
                        link(dve.memset(dA[:, :, :, 0:1], 0.0))
                        dve.wait_ge(bcast_used, i * 16 + 8)
                        dve.tensor_tensor_scan(h.rearrange("p n k -> p (n k)"),
                                               dA[:, :, :, :].rearrange("p n b t -> p (n b t)"),
                                               h.rearrange("p n k -> p (n k)"), 0.0, ALU.mult, ALU.add)\
                           .then_inc(scan_done, 1)
                        dve.wait_ge(scan_done, i + 1)
                    for pair in range(8):
                        j = i * 16 + half * 8 + pair
                        dve.wait_ge(bcast_ready, j + 1)
                        hn = h[:, 2 * pair:2 * pair + 2, :]
                        dve.tensor_tensor(hn, PS[:, 2 * (j % 2):2 * (j % 2) + 2, 0:QT],
                                          u2 if half == 0 else hn, ALU.mult).then_inc(bcast_used, 1)
            for q in range(NQ):
                dve.wait_ge(proj_ready, q + 1)
                dve.wait_ge(res_biased, q + 1)
                residual_norm(dve, link, q, [ps[4 + 2 * (q % 2) + i // 2][0:T, (i % 2) * D:(i % 2 + 1) * D]
                                             for i in range(QB)], proj_added)

        def residual_norm(dve, link, q, sources, used):
            for i, s in enumerate(sources):
                x = XA[0:T, q * QB + i, :]
                last = dve.tensor_tensor(x, s, x, ALU.add)
                last.then_inc(used, 1)
            residual_seen[used] = residual_seen.get(used, 0) + len(sources)
            dve.wait_ge(used, residual_seen[used])
            k = norm_stats(dve, link, [XA[0:T, q * QB + i, :] for i in range(QB)])
            for i in range(QB):
                x = XA[0:T, q * QB + i, :]
                last = norm_apply(dve, k, i, x, x)
            last.then_inc(norm_done, 1)

        residual_seen = {}

        def add_bias_rows(pool, name, norm_value):
            if norm_value:
                pool.wait_ge(norm_done, norm_value)
                pool.wait_ge(xt_ready, norm_value)
            for q in range(NQ):
                x = XA[0:T, q * QB:(q + 1) * QB, :]
                pool.tensor_tensor(x, x, row(name, T).unsqueeze(1).to_broadcast([T, QB, D]), ALU.add)\
                    .then_inc(res_biased, 1)

        def ssm_pool(pool, link):
            link(pool.memset(halves[:, :], -0.5))
            pool.wait_ge(x_loaded, 32)
            pool.wait_ge(const_loaded, 48)
            add_bias_rows(pool, "b_out", 0)
            for i in range(len(UNITS)):
                for pair in range(8):
                    h0, h1 = st_h[:, i % 2, 2 * pair, :], st_h[:, i % 2, 2 * pair + 1, :]
                    pool.wait_ge(bcast_used, i * 16 + 8 + pair + 1)
                    pool.tensor_tensor(h0, h0, h1, ALU.add).then_inc(pair_added, 1)
            for q in range(NQ):
                norm_root(pool, link, QB)

        H, HD = 16, 16
        HEADS = [(b, h) for b in range(B) for h in range(H)]
        ctx_loaded = [sem("ctx_loaded0"), sem("ctx_loaded1")]
        q_ready, q_copied = sem("q_ready"), sem("q_copied")
        k_ready, k_copied, v_ready, v_copied = sem("k_ready"), sem("k_copied"), sem("v_ready"), sem("v_copied")
        s_ready, max_ready, exp_done = sem("s_ready"), sem("max_ready"), sem("exp_done")
        pt_ready, pt_copied, av_done = sem("pt_ready"), sem("pt_copied"), sem("av_done")
        p_scaled, ot_copied, wo_loaded = sem("p_scaled"), sem("ot_copied"), sem("wo_loaded")
        S_BANK = (0, 1, 5)
        wo_ready, wo_added = sem("wo_ready"), sem("wo_added")

        def xat_load(sp):
            for b in range(B):
                if b == 0:
                    sp.wait_ge(xf_ready, 8)
                    sp.dma_start(wo4[:, :, :], dr["wo4"]).then_inc(wo_loaded, 16)
                if b >= 2:
                    sp.wait_ge(v_ready, 2 * (b - 1))
                for i in range(2):
                    sp.dma_start(ctx_t[0:CR[i], b % 2, i, :], dr["ctxT"][b, i * P:i * P + CR[i], :])\
                        .then_inc(ctx_loaded[b % 2], 16)
                if b == 2:
                    moe_load(sp)
            kernel_store(sp)

        def xat_banks():
            uses = [("q", i) for i in range(8)] + [("k", 0), ("k", 1), ("v", 0), ("v", 1)]
            for b in range(B + 1):
                if b >= 1:
                    uses += [("wo", b - 1)]
                if b >= 1 and b % QB == 0:
                    uses += [("xt", 2 * (b // QB) - 2), ("xt", 2 * (b // QB) - 1)]
                if b + 1 < B:
                    uses += [("k", 2 * b + 2), ("k", 2 * b + 3), ("v", 2 * b + 2), ("v", 2 * b + 3)]
            return {u: i for i, u in enumerate(uses)}, uses

        XAT_AT, XAT_USES = xat_banks()
        XAT_FREED = {"q": (q_copied, 0), "k": (k_copied, 0), "v": (v_copied, 0),
                     "wo": (wo_added, 0), "xt": (xf_ready, 8)}

        def xat_bank(kind, i):
            return 6 + XAT_AT[(kind, i)] % 2

        def xat_claim(pe, kind, i):
            n = XAT_AT[(kind, i)]
            if n >= 2:
                before, j = XAT_USES[n - 2]
                freed, base = XAT_FREED[before]
                pe.wait_ge(freed, base + j + 1)
            return ps[6 + n % 2]

        def xat_pe(pe):
            pe.wait_ge(wb_loaded, 16)
            pe.wait_ge(xf_ready, 8)
            for i, (c, q) in enumerate(UNITS):
                bank = xat_claim(pe, "q", i)
                for k in range(KC):
                    last = pe.matmul(bank[:, 0:QT], wb[:, k, c * P:(c + 1) * P], XF[:, k, q * QT:(q + 1) * QT],
                                     start=(k == 0), stop=(k == KC - 1))
                last.then_inc(q_ready, 1)

            def keys(b):
                pe.wait_ge(ctx_loaded[b % 2], 32 * (b // 2 + 1))
                for c in range(KC):
                    bank = xat_claim(pe, "k", 2 * b + c)
                    for i in range(2):
                        last = pe.matmul(bank[:, 0:S2], wb[0:CR[i], i, D + c * P:D + (c + 1) * P],
                                         ctx_t[0:CR[i], b % 2, i, :], start=(i == 0), stop=(i == 1))
                    last.then_inc(k_ready, 1)

            def values(b):
                for part, chunks_ in enumerate(((0, 1), (2,))):
                    bank = xat_claim(pe, "v", 2 * b + part)
                    for m, j in enumerate(chunks_):
                        for i in range(2):
                            last = pe.matmul(bank[0:JR, m * D:(m + 1) * D],
                                             ctx_t[0:CR[i], b % 2, i, j * JR:(j + 1) * JR],
                                             wb[0:CR[i], i, 2 * D:3 * D], start=(i == 0), stop=(i == 1))
                    last.then_inc(v_ready, 1)

            def scores(g):
                b, h = HEADS[g]
                if g == 0:
                    pe.wait_ge(q_copied, 8)
                if h == 0:
                    pe.wait_ge(k_copied, 2 * b + 2)
                if g >= 3:
                    pe.wait_ge(exp_done, g - 2)
                r = slice(32 * (h % 8 // 2), 32 * (h % 8 // 2) + 32)
                pe.matmul(ps[S_BANK[g % 3]][0:T, 0:S2], qm[r, h % 2, h // 8, b * T:(b + 1) * T],
                          k_t[r, b % 2, h // 8, :], start=True, stop=True).then_inc(s_ready, 1)

            def turn(g):
                pe.wait_ge(p_scaled, g + 1)
                if g >= 2:
                    pe.wait_ge(pt_copied, g - 1)
                for j in range(JC):
                    last = pe.transpose(ps[2 + g % 2][0:JR, j * T:(j + 1) * T],
                                        prob[0:T, g % 3, j * JR:(j + 1) * JR], ident[0:T, 0:T])
                last.then_inc(pt_ready, 1)

            def weigh(g):
                b, h = HEADS[g]
                if h == 0:
                    pe.wait_ge(v_copied, 2 * b + 2)
                    if b >= 1:
                        pe.wait_ge(ot_copied, b)
                pe.wait_ge(pt_copied, g + 1)
                for j in range(JC):
                    last = pe.matmul(ps[4][32 * (h % 4):32 * (h % 4) + 32, h // 4 * T:(h // 4 + 1) * T],
                                     v_t[0:JR, b % 2, j, 2 * HD * (h // 2):2 * HD * (h // 2 + 1)],
                                     prob_t[0:JR, g % 2, j, :],
                                     start=(j == 0), stop=(j == JC - 1))
                last.then_inc(av_done, 1)

            def project(b):
                bank = xat_claim(pe, "wo", b)
                pe.wait_ge(ot_copied, b + 1)
                if b == 0:
                    pe.wait_ge(wo_loaded, 16)
                for k in range(4):
                    last = pe.matmul(bank[0:T, 0:D], o_t[:, b % 2, k, :], wo4[:, k, :],
                                     start=(k == 0), stop=(k == 3))
                last.then_inc(wo_ready, 1)

            def turn_residual(q):
                pe.wait_ge(norm_done, 4 + q + 1)
                for c in range(KC):
                    bank = xat_claim(pe, "xt", 2 * q + c)
                    for i in range(QB):
                        last = pe.transpose(bank[:, i * T:(i + 1) * T],
                                            XA[0:T, q * QB + i, c * P:(c + 1) * P], ident[0:T, 0:T])
                last.then_inc(xt_ready, 1)

            keys(0)
            values(0)
            scores(0)
            scores(1)
            for g in range(len(HEADS) + 8):
                b, h = divmod(g, H)
                if g + 2 < len(HEADS):
                    scores(g + 2)
                if g < len(HEADS):
                    turn(g)
                if 1 <= g <= len(HEADS):
                    weigh(g - 1)
                if b >= 1 and h == 3:
                    project(b - 1)
                if b >= 1 and b % QB == 0 and h == 7:
                    turn_residual(b // QB - 1)
                if h == 8 and b + 1 < B:
                    keys(b + 1)
                if h == 10 and b + 1 < B:
                    values(b + 1)

        def xat_act(act):
            act.wait_ge(scaled, 2)
            kernel_act_dt(act)
            for i, (c, q) in enumerate(UNITS):
                act.wait_ge(q_ready, i + 1)
                for par in range(2):
                    last = act.activation(qm[:, par, c, q * QT:(q + 1) * QT], ps[xat_bank("q", i)][:, 0:QT],
                                          ACT.Identity, bias=bq_m[:, par, c:c + 1],
                                          scale=col("head_mask", i=par))
                last.then_inc(q_copied, 1)

            def copy_keys(b):
                for c in range(KC):
                    act.wait_ge(k_ready, 2 * b + c + 1)
                    act.activation(k_t[:, b % 2, c, :], ps[xat_bank("k", 2 * b + c)][:, 0:S2], ACT.Identity,
                                   bias=col("bk", i=c)).then_inc(k_copied, 1)

            def exponents(g):
                act.wait_ge(max_ready, g + 1)
                if g >= 3:
                    act.wait_ge(pt_ready, g - 2)
                act.activation(prob[0:T, g % 3, :], ps[S_BANK[g % 3]][0:T, 0:S2], ACT.Exp,
                               bias=nmax[0:T, g % 4:g % 4 + 1],
                               accum_out=sums[0:T, g % 4:g % 4 + 1]).then_inc(exp_done, 1)

            copy_keys(0)
            exponents(0)
            for g in range(len(HEADS) + 8):
                b, h = divmod(g, H)
                if g + 1 < len(HEADS):
                    exponents(g + 1)
                if g < len(HEADS):
                    act.wait_ge(pt_ready, g + 1)
                    if g >= 2:
                        act.wait_ge(av_done, g - 1)
                    act.copy(prob_t[0:JR, g % 2, :, :].rearrange("p j t -> p (j t)"),
                             ps[2 + g % 2][0:JR, 0:JC * T]).then_inc(pt_copied, 1)
                if b >= 1 and h == 0:
                    act.wait_ge(av_done, H * b)
                    if b >= 3:
                        act.wait_ge(wo_ready, b - 2)
                    act.copy(o_t[:, (b - 1) % 2, :, :].rearrange("p c t -> p (c t)"),
                             ps[4][:, 0:4 * T]).then_inc(ot_copied, 1)
                if b >= 1 and b % QB == 0 and h == 7:
                    q = b // QB - 1
                    act.wait_ge(xt_ready, 4 + q + 1)
                    for c in range(KC):
                        act.copy(XF[:, c, q * QT:(q + 1) * QT],
                                 ps[xat_bank("xt", 2 * q + c)][:, 0:QT]).then_inc(xf_ready, 1)
                if h == 8 and b + 1 < B:
                    copy_keys(b + 1)
                if g == 24:
                    kernel_act_trig(act)

        def xat_dve(dve, link):
            for par in range(2):
                last = dve.tensor_scalar(bq_m[:, par, :], cols[:, COLS.at["bq"][0]:COLS.at["bq"][0] + KC],
                                         col("head_mask", i=par), None, ALU.mult)
            last.then_inc(scaled, 1)

            def row_max(g):
                dve.wait_ge(s_ready, g + 1)
                if g >= 4:
                    dve.wait_ge(exp_done, g - 3)
                dve.tensor_reduce(nmax[0:T, g % 4:g % 4 + 1], ps[S_BANK[g % 3]][0:T, 0:S2], AX.X, ALU.max,
                                  negate=True).then_inc(max_ready, 1)

            def copy_values(b):
                for part, (m, j) in enumerate(((2, 0), (1, 2))):
                    dve.wait_ge(v_ready, 2 * b + part + 1)
                    if b >= 2:
                        dve.wait_ge(av_done, H * (b - 1))
                    dve.tensor_tensor(v_t[0:JR, b % 2, j:j + m, :],
                                      ps[xat_bank("v", 2 * b + part)][0:JR, 0:m * D].rearrange(
                                          "p (m d) -> p m d", d=D),
                                      row("bv", JR).unsqueeze(1).to_broadcast([JR, m, D]), ALU.add)\
                        .then_inc(v_copied, 1)

            def divide(g):
                dve.wait_ge(exp_done, g + 1)
                s = sums[0:T, g % 4:g % 4 + 1]
                link(dve.reciprocal(s, s))
                dve.tensor_scalar(prob[0:T, g % 3, :], prob[0:T, g % 3, :], s, None, ALU.mult).then_inc(p_scaled, 1)

            row_max(0)
            row_max(1)
            copy_values(0)
            divide(0)
            for g in range(len(HEADS) + 8):
                b, h = divmod(g, H)
                if g + 2 < len(HEADS):
                    row_max(g + 2)
                if g + 1 < len(HEADS):
                    divide(g + 1)
                if b >= 1 and h == 5:
                    dve.wait_ge(wo_ready, b)
                    if b == 1:
                        dve.wait_ge(res_biased, 8)
                    dve.tensor_tensor(XA[0:T, b - 1, :], ps[xat_bank("wo", b - 1)][0:T, 0:D],
                                      XA[0:T, b - 1, :], ALU.add).then_inc(wo_added, 1)
                    if b % QB == 0:
                        dve.wait_ge(wo_added, b)
                        norm_rows(dve, link, b // QB - 1)
                if h == 11 and b + 1 < B:
                    copy_values(b + 1)

        def norm_rows(dve, link, q):
            k = norm_stats(dve, link, [XA[0:T, q * QB + i, :] for i in range(QB)])
            for i in range(QB):
                x = XA[0:T, q * QB + i, :]
                last = norm_apply(dve, k, i, x, x)
            last.then_inc(norm_done, 1)

        def xat_pool(pool, link):
            add_bias_rows(pool, "bo", 4)
            pool.wait_ge(xf_ready, 8)
            kernel_setup(pool, link)
            for q in range(NQ):
                for unit in range(4 * q, min(4 * q + 4, KC * KHIGH)):
                    kernel_lags(pool, link, unit)
                if q == NQ - 1:
                    kernel_end(pool, link)
                norm_root(pool, link, QB)

        FILL = -3e38
        w1_e = wc[:, 0:E8 * KC * D].rearrange("p (e k d) -> p e k d", e=E8, k=KC)
        w2_e = wc[:, E8 * KC * D:2 * E8 * KC * D].rearrange("p (e k d) -> p e k d", e=E8, k=KC)
        moe_loaded, gate_loaded = sem("moe_loaded"), sem("gate_loaded")
        gate_ready, gate_done, gt_ready, gt_copied = (
            sem("gate_ready"), sem("gate_done"), sem("gt_ready"), sem("gt_copied"))
        h_ready, h_done, y_out, y_added = sem("h_ready"), sem("h_done"), sem("y_out"), sem("y_added")

        def moe_load(sp):
            sp.dma_start(wc[:, :], dr["wc"]).then_inc(moe_loaded, 16)

        def moe_small_load(sp):
            sp.wait_ge(xf_ready, 16)
            sp.dma_start(moe_small[:, :], dr["moe_gate"]).then_inc(gate_loaded, 16)
            sp.dma_start(moe_b2[:, :], dr["moe_b2"]).then_inc(gate_loaded, 16)

        def moe_pairs():
            uses = []
            for i in range(NQ * E8):
                uses.append(("h", i))
                if i % E8 == 1 and i > E8:
                    uses.append(("xt", i // E8 - 1))
            uses.append(("xt", NQ - 1))
            return uses, {u: n for n, u in enumerate(uses)}

        MOE_USES, MOE_AT = moe_pairs()

        def moe_pair(kind, i):
            return 2 * (MOE_AT[(kind, i)] % 2)

        def moe_claim(pe, kind, i):
            n = MOE_AT[(kind, i)]
            if n >= 2:
                before, j = MOE_USES[n - 2]
                if before == "h":
                    pe.wait_ge(h_done, KC * (j + 1))
                else:
                    pe.wait_ge(xf_ready, 16 + 2 * (j + 1))
            return 2 * (n % 2)

        def moe_pe(pe):
            pe.wait_ge(gate_loaded, 32)
            pe.wait_ge(xf_ready, 16)
            for b in range(B):
                for k in range(KC):
                    last = pe.matmul(ps[0][0:T, b * E8:(b + 1) * E8], XF[:, k, b * T:(b + 1) * T],
                                     moe_small[:, k * E8:(k + 1) * E8], start=(k == 0), stop=(k == KC - 1))
            last.then_inc(gate_ready, 1)
            pe.wait_ge(gate_done, 1)
            for q in range(NQ):
                for i in range(QB):
                    last = pe.transpose(ps[q][0:E8, i * T:(i + 1) * T], gate_w[0:T, q * QB + i, :],
                                        ident[0:T, 0:T])
                last.then_inc(gt_ready, 1)
            pe.wait_ge(gt_copied, NQ)
            pe.wait_ge(moe_loaded, 16)

            def hidden(i):
                q, e = divmod(i, E8)
                pair = moe_claim(pe, "h", i)
                for m in range(KC):
                    for k in range(KC):
                        last = pe.matmul(ps[pair + m][:, 0:QT], w1_e[:, e, k, m * P:(m + 1) * P],
                                         XF[:, k, q * QT:(q + 1) * QT], start=(k == 0), stop=(k == KC - 1))
                last.then_inc(h_ready, 1)

            def claim_y(j, i):
                if j >= 1:
                    pe.wait_ge(y_added, QB * (j - 1) + i + 1)
                return ps[4 + i][0:T, 0:D]

            def outputs(i):
                q, e = divmod(i, E8)
                if e == 0:
                    for b in range(QB):
                        bank = claim_y(9 * q, b)
                        t = (q * QB + b) * T
                        pe.matmul(bank, gate_wt[:, t:t + T], moe_b2[:, :], start=True, stop=True)\
                            .then_inc(y_out, 1)
                pe.wait_ge(h_done, KC * (i + 1))
                for b in range(QB):
                    bank = claim_y(9 * q + e + 1, b)
                    for k in range(KC):
                        last = pe.matmul(bank, h_t[:, i % 2, k, b * T:(b + 1) * T], w2_e[:, e, k, :],
                                         start=(k == 0), stop=(k == KC - 1))
                    last.then_inc(y_out, 1)

            def turn(q):
                pair = moe_claim(pe, "xt", q)
                transposed_to_features(pe, q, pair, 8 + q + 1)

            for i in range(NQ * E8 + 1):
                if i < NQ * E8:
                    hidden(i)
                if i >= 1:
                    outputs(i - 1)
                if i % E8 == 1 and i > E8:
                    turn(i // E8 - 1)
            turn(NQ - 1)

        def moe_act(act):
            for i in range(NQ * E8):
                q, e = divmod(i, E8)
                act.wait_ge(h_ready, i + 1)
                if i >= 2:
                    qq, ee = divmod(i - 2, E8)
                    act.wait_ge(y_out, QB * (9 * qq + ee + 2))
                for m in range(KC):
                    act.activation(h_t[:, i % 2, m, :], ps[moe_pair("h", i) + m][:, 0:QT], ACT.Relu,
                                   bias=col("moe_b1", i=KC * e + m)).then_inc(h_done, 1)
                if i % E8 == 1 and i > E8:
                    copy_features(act, q - 1, moe_pair("xt", q - 1), 8 + q, XD)
            copy_features(act, NQ - 1, moe_pair("xt", NQ - 1), 8 + NQ, XD)

        def moe_dve(dve, link):
            dve.wait_ge(xf_ready, 16)
            dve.memset(gate_s[:, :, :], FILL)
            link(dve.memset(gate_p[:, :, :], FILL))
            dve.wait_ge(gate_ready, 1)
            link(dve.tensor_tensor(gate_s[0:T, :, 0:E8],
                                   ps[0][0:T, 0:B * E8].rearrange("p (b e) -> p b e", e=E8),
                                   row("moe_bg", T).unsqueeze(1).to_broadcast([T, B, E8]), ALU.add))
            for b in range(B):
                last = dve.max(gate_m[0:T, b, :], gate_s[0:T, b, :])
            link(last)
            link(dve.tensor_copy(gate_p[0:T, :, 0:2], gate_m[0:T, :, 0:2]))
            for b in range(B):
                last = dve.match_replace(gate_r[0:T, b, :], gate_p[0:T, b, :], gate_s[0:T, b, :], -FILL)
            link(last)
            link(dve.tensor_tensor(gate_r[0:T, :, 0:E8], gate_r[0:T, :, 0:E8], gate_s[0:T, :, 0:E8],
                                   ALU.not_equal))
            dve.tensor_tensor(gate_w[0:T, :, :], gate_r[0:T, :, 0:E8], gate_s[0:T, :, 0:E8], ALU.mult)\
                .then_inc(gate_done, 1)
            for q in range(NQ):
                dve.wait_ge(gt_ready, q + 1)
                dve.tensor_copy(gate_wt[:, q * QT:(q + 1) * QT], ps[q][0:E8, 0:QT]).then_inc(gt_copied, 1)
            dve.wait_ge(gate_done, 1)
            for q in range(NQ):
                for j in range(9):
                    for i in range(QB):
                        b = q * QB + i
                        n = QB * (9 * q + j) + i
                        x = XA[0:T, b, :]
                        dve.wait_ge(y_out, n + 1)
                        if j:
                            dve.wait_ge(y_added, n - QB + 1)
                            last = dve.scalar_tensor_tensor(x, ps[4 + i][0:T, 0:D], gate_w[0:T, b, j - 1:j], x,
                                                            ALU.mult, ALU.add)
                        else:
                            last = dve.tensor_tensor(x, ps[4 + i][0:T, 0:D], x, ALU.add)
                        last.then_inc(y_added, 1)
                dve.wait_ge(y_added, QB * 9 * (q + 1))
                norm_rows(dve, link, q)

        def moe_pool(pool, link):
            for q in range(NQ):
                norm_root(pool, link, QB)

        STEPS = LAYERS * ROUNDS
        xg = XG[:, 0:2 * ROUNDS * D].rearrange("p (g d) -> p g d", d=D)
        enc_loaded = [sem("enc_loaded0"), sem("enc_loaded1")]
        (xg0_turned, xg0_copied, eq_ready, eq_copied, ek_copied, ev_ready, ev_copied, qx_ready,
         es_ready, es_used, ee_done, ep_ready, et_ready, px_ready, ea_ready, eu_copied,
         ew_ready, ew_added, n1_done, ex_ready, x1f_copied, x1_biased, f1_ready, f2_ready, relu1, relu2,
         eg_ready, eg_added, n2_done, ez_ready, ez_copied, xg_biased, xa_turned, xa_copied) = (
            sem(n) for n in (
                "xg0_turned xg0_copied eq_ready eq_copied ek_copied ev_ready ev_copied qx_ready "
                "es_ready es_used ee_done ep_ready et_ready px_ready ea_ready eu_copied "
                "ew_ready ew_added n1_done ex_ready x1f_copied x1_biased f1_ready f2_ready relu1 relu2 "
                "eg_ready eg_added n2_done ez_ready ez_copied xg_biased xa_turned xa_copied").split())

        def enc_w(layer):
            w = enc_w0[:, :] if layer % 2 == 0 else wc[:, 0:ENC_W]
            return (w[:, 0:1536].rearrange("p (k n) -> p k n", k=KC),
                    w[:, 1536:2560].rearrange("p (k n) -> p k n", k=4),
                    w[:, 2560:4608].rearrange("p (k n) -> p k n", k=KC),
                    w[:, 4608:6656].rearrange("p (k n) -> p k n", k=8))

        def enc_row(layer, name):
            return enc_rows[:, layer % 2, ENC_ROWS.index(name):ENC_ROWS.index(name) + 1, :]\
                .to_broadcast([P, 2, D])

        def enc_wait_layer(eng, layer):
            eng.wait_ge(enc_loaded[layer % 2], 32 * (layer // 2 + 1))

        def enc_first_load(sp):
            sp.wait_ge(wo_ready, B)
            sp.dma_start(enc_w0[:, :], dr["enc_w"][0]).then_inc(enc_loaded[0], 16)

        def enc_load(sp):
            sp.wait_ge(xf_ready, 24)
            sp.dma_start(enc_rows[:, 0, :, :], dr["enc_rows"][0].partition_broadcast(P))\
                .then_inc(enc_loaded[0], 16)
            for layer in range(1, LAYERS):
                if layer >= 2:
                    sp.wait_ge(n2_done, ROUNDS * (layer - 1))
                if layer % 2:
                    dst = wc[:, 0:ENC_W]
                else:
                    dst = enc_w0[:, :]
                sp.dma_start(dst, dr["enc_w"][layer]).then_inc(enc_loaded[layer % 2], 16)
                sp.dma_start(enc_rows[:, layer % 2, :, :], dr["enc_rows"][layer].partition_broadcast(P))\
                    .then_inc(enc_loaded[layer % 2], 16)

        def enc_pe(pe):
            pe.wait_ge(xf_ready, 24)
            for r in range(ROUNDS):
                if r >= 2:
                    pe.wait_ge(xg0_copied, r - 1)
                for g in range(2):
                    for c in range(KC):
                        last = pe.transpose(ps[r % 2][:, g * D + c * P:g * D + (c + 1) * P],
                                            XD[:, c, r * RT + g * P:r * RT + (g + 1) * P], ident[:, :])
                last.then_inc(xg0_turned, 1)
            pe.wait_ge(xg0_copied, ROUNDS)

            def turn(bank, src):
                for c in range(KC):
                    for g in range(2):
                        last = pe.transpose(ps[bank][:, c * RT + g * P:c * RT + (g + 1) * P],
                                            src[:, g, c * P:(c + 1) * P], ident[:, :])
                return last

            def qkv(i):
                layer, r = divmod(i, ROUNDS)
                w = enc_w(layer)[0]
                if r == 0:
                    enc_wait_layer(pe, layer)
                if layer >= 1:
                    pe.wait_ge(ez_copied, i - ROUNDS + 1)
                if i >= 3:
                    pe.wait_ge(relu2, i - 2)
                elif i >= 1:
                    pe.wait_ge(ek_copied, i)
                t = slice(r * RT, (r + 1) * RT)
                for j in range(2):
                    for c in range(KC):
                        for k in range(KC):
                            last = pe.matmul(ps[4 + j][:, c * RT:(c + 1) * RT],
                                             w[:, k, j * D + c * P:j * D + (c + 1) * P], XD[:, k, t],
                                             start=(k == 0), stop=(k == KC - 1))
                    last.then_inc(eq_ready, 1)
                if i >= 2:
                    pe.wait_ge(ew_added, i - 1)
                elif i == 1:
                    pe.wait_ge(ev_copied, 1)
                for g in range(2):
                    for k in range(KC):
                        last = pe.matmul(ps[6][:, g * D:(g + 1) * D],
                                         XD[:, k, r * RT + g * P:r * RT + (g + 1) * P], w[:, k, 2 * D:3 * D],
                                         start=(k == 0), stop=(k == KC - 1))
                last.then_inc(ev_ready, 1)

            def scores(i):
                pe.wait_ge(qx_ready, i + 1)
                pe.wait_ge(ek_copied, i + 1)
                if i >= 2:
                    pe.wait_ge(relu1, i - 1)
                for t in range(16):
                    for c in range(KC):
                        at = t // 8 * 256 + c * P + t % 8 * 16
                        last = pe.matmul(ps[0][:, at:at + 16], q_x[:, c, t, :],
                                         k_f[:, i % 2, c, t * 16:(t + 1) * 16], start=True, stop=True)
                last.then_inc(es_ready, 1)

            def turn_probs(i):
                pe.wait_ge(ep_ready, i + 1)
                if i >= 1:
                    pe.wait_ge(px_ready, i)
                for m in range(4):
                    last = pe.transpose(ps[1][:, m * P:(m + 1) * P],
                                        s_m[:, 8 * m:8 * m + 8, :].rearrange("p t j -> p (t j)"), ident[:, :])
                last.then_inc(et_ready, 1)

            def weigh(i):
                pe.wait_ge(px_ready, i + 1)
                pe.wait_ge(ev_copied, i + 1)
                if i >= 1:
                    pe.wait_ge(x1f_copied, i)
                if i >= 2:
                    pe.wait_ge(ez_copied, i - 1)
                for g in range(2):
                    for h in range(16):
                        last = pe.matmul(
                            ps[2 + g][32 * (h % 4):32 * (h % 4) + 32, h // 4 * P:(h // 4 + 1) * P],
                            v_g[:, i % 2, g, 32 * (h // 2):32 * (h // 2) + 32],
                            p_x[:, 2 * g + h // 8, h % 8, :, :].rearrange("p t i -> p (t i)"),
                            start=True, stop=True)
                last.then_inc(ea_ready, 1)

            def feed_in(i, half):
                w = enc_w(i // ROUNDS)[2]
                if half == 0:
                    pe.wait_ge(x1f_copied, i + 1)
                    if i + 1 < STEPS:
                        pe.wait_ge(es_used, i + 2)
                    if i >= 1:
                        pe.wait_ge(relu1, i)
                else:
                    if i + 2 < STEPS:
                        pe.wait_ge(eq_copied, i + 3)
                        pe.wait_ge(ek_copied, i + 3)
                    if i >= 1:
                        pe.wait_ge(relu2, i)
                for m in range(4 * half, 4 * half + 4):
                    bank = (7, 0, 4, 5)[m // 2]
                    for k in range(KC):
                        last = pe.matmul(ps[bank][:, (m % 2) * RT:(m % 2 + 1) * RT], w[:, k, m * P:(m + 1) * P],
                                         x1f[:, i % 2, k, :], start=(k == 0), stop=(k == KC - 1))
                last.then_inc((f1_ready, f2_ready)[half], 1)

            def feed_out(i):
                w = enc_w(i // ROUNDS)[3]
                pe.wait_ge(relu1, i + 1)
                pe.wait_ge(relu2, i + 1)
                if i + 2 < STEPS:
                    pe.wait_ge(ev_copied, i + 3)
                pe.wait_ge(ew_added, i + 1)
                for g in range(2):
                    for m in range(8):
                        last = pe.matmul(ps[6][:, g * D:(g + 1) * D], h_ff[:, m, g * P:(g + 1) * P], w[:, m, :],
                                         start=(m == 0), stop=(m == 7))
                last.then_inc(eg_ready, 1)

            def project(i):
                w = enc_w(i // ROUNDS)[1]
                pe.wait_ge(eu_copied, i + 1)
                if i >= 1:
                    pe.wait_ge(eg_added, i)
                elif STEPS > 1:
                    pe.wait_ge(ev_copied, 2)
                for g in range(2):
                    for k in range(4):
                        last = pe.matmul(ps[6][:, g * D:(g + 1) * D], o_f[:, g, k, :], w[:, k, :],
                                         start=(k == 0), stop=(k == 3))
                last.then_inc(ew_ready, 1)

            for k in range(STEPS + 3):
                if 0 <= k - 1 < STEPS:
                    scores(k - 1)
                if 0 <= k - 2 < STEPS:
                    pe.wait_ge(n1_done, k - 1)
                    turn(2, x1[:, k % 2, :, :]).then_inc(ex_ready, 1)
                if 0 <= k - 3 < STEPS:
                    i = k - 3
                    pe.wait_ge(n2_done, i + 1)
                    if i + 1 < STEPS:
                        pe.wait_ge(eu_copied, i + 2)
                    if i >= 1:
                        pe.wait_ge(ez_copied, i)
                    r = i % ROUNDS
                    turn(3, xg[:, 2 * r:2 * r + 2, :]).then_inc(ez_ready, 1)
                if k < STEPS:
                    qkv(k)
                if 0 <= k - 1 < STEPS:
                    turn_probs(k - 1)
                if 0 <= k - 2 < STEPS:
                    feed_in(k - 2, 0)
                if 0 <= k - 1 < STEPS:
                    weigh(k - 1)
                if 0 <= k - 2 < STEPS:
                    feed_in(k - 2, 1)
                if 0 <= k - 2 < STEPS:
                    feed_out(k - 2)
                if 0 <= k - 1 < STEPS:
                    project(k - 1)
            pe.wait_ge(ez_copied, STEPS)
            for j in range(B // 2):
                if j >= 2:
                    pe.wait_ge(xa_copied, j - 1)
                for m in range(2):
                    for c in range(KC):
                        last = pe.transpose(ps[j % 2][0:T, m * D + c * P:m * D + (c + 1) * P],
                                            XF[:, c, (2 * j + m) * T:(2 * j + m + 1) * T], ident[:, :])
                last.then_inc(xa_turned, 1)

        def enc_act(act):
            for r in range(ROUNDS):
                act.wait_ge(xg0_turned, r + 1)
                act.copy(xg0[:, 2 * r:2 * r + 2, :].rearrange("p g d -> p (g d)"), ps[r % 2])\
                    .then_inc(xg0_copied, 1)
            act.wait_ge(scaled, 3)
            for k in range(STEPS + 3):
                if 0 <= k - 2 < STEPS:
                    act.wait_ge(ex_ready, k - 1)
                    act.copy(x1f[:, k % 2, :, :].rearrange("p c n -> p (c n)"), ps[2]).then_inc(x1f_copied, 1)
                if 0 <= k - 3 < STEPS:
                    layer, r = divmod(k - 3, ROUNDS)
                    act.wait_ge(ez_ready, k - 2)
                    src = ps[3].rearrange("p (c n) -> p c n", c=KC)
                    if layer < LAYERS - 1:
                        act.copy(XD[:, :, r * RT:(r + 1) * RT], src).then_inc(ez_copied, 1)
                    else:
                        for c in range(KC):
                            last = act.copy(
                                XF[:, c, :].rearrange("p (b t) -> p t b", b=B)[:, 16 * r:16 * r + 16, :],
                                src[:, c, :].rearrange("p (t b) -> p t b", b=B))
                        last.then_inc(ez_copied, 1)
                if 0 <= k - 1 < STEPS:
                    act.wait_ge(es_used, k)
                    act.activation(s_m[:, :, :], s_m[:, :, :], ACT.Exp).then_inc(ee_done, 1)
                if k < STEPS:
                    layer = k // ROUNDS
                    for j, (dst, copied) in enumerate(((q_f, eq_copied), (k_f, ek_copied))):
                        act.wait_ge(eq_ready, 2 * k + j + 1)
                        for c in range(KC):
                            last = act.activation(
                                dst[:, k % 2, c, :], ps[4 + j][:, c * RT:(c + 1) * RT], ACT.Identity,
                                bias=col("enc_bk", i=2 * layer + c) if j else bq4[:, 2 * layer + c:2 * layer + c + 1],
                                scale=1.0 if j else 0.25)
                        last.then_inc(copied, 1)

                def relu(half):
                    i = k - 2
                    act.wait_ge((f1_ready, f2_ready)[half], i + 1)
                    for m in range(4 * half, 4 * half + 4):
                        last = act.activation(h_ff[:, m, :],
                                              ps[(7, 0, 4, 5)[m // 2]][:, (m % 2) * RT:(m % 2 + 1) * RT],
                                              ACT.Relu, bias=col("enc_b1", i=8 * (i // ROUNDS) + m))
                    last.then_inc((relu1, relu2)[half], 1)

                if 0 <= k - 2 < STEPS:
                    relu(0)
                if 0 <= k - 1 < STEPS:
                    act.wait_ge(ea_ready, k)
                    if k >= 2:
                        act.wait_ge(ew_ready, k - 1)
                    act.copy(o_f[:, :, :, :].rearrange("p g c n -> p g (c n)"), PS[:, 2:4, :]).then_inc(eu_copied, 1)
                if 0 <= k - 2 < STEPS:
                    relu(1)
            for j in range(B // 2):
                act.wait_ge(xa_turned, j + 1)
                act.copy(XA[0:T, 2 * j:2 * j + 2, :].rearrange("p b d -> p (b d)"), ps[j % 2][0:T, :])\
                    .then_inc(xa_copied, 1)

        def enc_dve(dve, link):
            a, w = COLS.at["enc_bq"]
            dve.wait_ge(xf_ready, 24)
            dve.tensor_scalar(bq4[:, :], cols[:, a:a + w], 0.25, None, ALU.mult).then_inc(scaled, 1)

            def affine(layer, tile, g, b, done):
                link(dve.tensor_tensor(tile, tile, enc_row(layer, g), ALU.mult))
                ins = dve.tensor_tensor(tile, tile, enc_row(layer, b), ALU.add)
                if done is None:
                    link(ins)
                else:
                    ins.then_inc(done, 1)

            def normed(tile):
                k = norm_stats(dve, link, [tile[:, g, :] for g in range(2)], P)
                for g in range(2):
                    last = norm_apply(dve, k, g, tile[:, g, :], tile[:, g, :], P)
                return last

            for k in range(STEPS + 2):
                if 0 <= k - 1 < STEPS:
                    i = k - 1
                    s = ps[0].rearrange("p (m j) -> p m j", j=16)
                    dve.wait_ge(es_ready, i + 1)
                    link(dve.tensor_reduce(s_x[:, :], s, AX.X, ALU.max))
                    if i >= 1:
                        dve.wait_ge(et_ready, i)
                    dve.tensor_tensor(s_m[:, :, :], s, s_x[:, :].unsqueeze(2).to_broadcast([P, 32, 16]),
                                      ALU.subtract).then_inc(es_used, 1)
                    dve.wait_ge(ee_done, i + 1)
                    link(dve.tensor_reduce(s_s[:, :], s_m[:, :, :], AX.X, ALU.add))
                    link(dve.reciprocal(s_s[:, :], s_s[:, :]))
                    dve.tensor_tensor(s_m[:, :, :], s_m[:, :, :],
                                      s_s[:, :].unsqueeze(2).to_broadcast([P, 32, 16]), ALU.mult)\
                        .then_inc(ep_ready, 1)
                if k < STEPS:
                    layer, r = divmod(k, ROUNDS)
                    if r == 0:
                        enc_wait_layer(dve, layer)
                    dve.wait_ge(ev_ready, k + 1)
                    dve.tensor_tensor(v_g[:, k % 2, :, :], ps[6].rearrange("p (g d) -> p g d", d=D),
                                      enc_row(layer, "bv"), ALU.add).then_inc(ev_copied, 1)
                if 0 <= k - 1 < STEPS:
                    dve.wait_ge(et_ready, k)
                    for m in range(4):
                        last = dve.tensor_tensor(
                            p_x[:, m, :, :, :],
                            ps[1][:, m * P:(m + 1) * P].rearrange("p (h i) -> p h i", i=16).unsqueeze(2)
                            .to_broadcast([P, 8, 8, 16]),
                            diag8.unsqueeze(1).unsqueeze(3).to_broadcast([P, 8, 8, 16]), ALU.mult)
                    last.then_inc(px_ready, 1)
                if 0 <= k - 2 < STEPS:
                    i = k - 2
                    layer, r = divmod(i, ROUNDS)
                    x = xg[:, 2 * r:2 * r + 2, :]
                    dve.wait_ge(x1_biased, i + 1)
                    dve.wait_ge(eg_ready, i + 1)
                    dve.tensor_tensor(x, ps[6].rearrange("p (g d) -> p g d", d=D), x1[:, i % 2, :, :], ALU.add)\
                        .then_inc(eg_added, 1)
                    dve.wait_ge(eg_added, i + 1)
                    link(normed(x))
                    if layer < LAYERS - 1:
                        affine(layer, x, "g2", "be2", n2_done)
                    else:
                        affine(layer, x, "g2", "be2", None)
                        link(dve.tensor_tensor(x, x, xg0[:, 2 * r:2 * r + 2, :], ALU.add))
                        normed(x).then_inc(n2_done, 1)
                if 0 <= k - 1 < STEPS:
                    i = k - 1
                    layer, r = divmod(i, ROUNDS)
                    x = x1[:, i % 2, :, :]
                    dve.wait_ge(xg_biased, i + 1)
                    dve.wait_ge(ew_ready, i + 1)
                    dve.tensor_tensor(x, ps[6].rearrange("p (g d) -> p g d", d=D), xg[:, 2 * r:2 * r + 2, :],
                                      ALU.add).then_inc(ew_added, 1)
                    dve.wait_ge(ew_added, i + 1)
                    link(normed(x))
                    affine(layer, x, "g1", "be1", n1_done)

        diag8 = cols[:, COLS.at["diag8"][0]:COLS.at["diag8"][0] + 8]

        def enc_pool(pool, link):
            enc_wait_layer(pool, 0)
            for r in range(ROUNDS):
                pool.wait_ge(xg0_copied, r + 1)
                pool.tensor_tensor(xg[:, 2 * r:2 * r + 2, :], xg0[:, 2 * r:2 * r + 2, :], enc_row(0, "bo"),
                                   ALU.add).then_inc(xg_biased, 1)
            for k in range(STEPS + 3):
                if 0 <= k - 2 < STEPS:
                    x = x1[:, k % 2, :, :]
                    pool.wait_ge(ex_ready, k - 1)
                    pool.tensor_tensor(x, x, enc_row((k - 2) // ROUNDS, "b2"), ALU.add).then_inc(x1_biased, 1)
                if 0 <= k - 3 < STEPS - ROUNDS:
                    layer, r = divmod(k - 3, ROUNDS)
                    if r == 0:
                        enc_wait_layer(pool, layer + 1)
                    x = xg[:, 2 * r:2 * r + 2, :]
                    pool.wait_ge(ez_ready, k - 2)
                    pool.tensor_tensor(x, x, enc_row(layer + 1, "bo"), ALU.add).then_inc(xg_biased, 1)
                if k < STEPS:
                    pool.wait_ge(eq_copied, k + 1)
                    if k >= 1:
                        pool.wait_ge(es_ready, k)
                    for c in range(KC):
                        last = pool.tensor_tensor(
                            q_x[:, c, :, :].rearrange("p t (h i) -> p t h i", i=16),
                            q_f[:, k % 2, c, :].rearrange("p (t i) -> p t i", i=16).unsqueeze(2)
                            .to_broadcast([P, 16, 8, 16]),
                            diag8.unsqueeze(1).unsqueeze(3).to_broadcast([P, 16, 8, 16]), ALU.mult)
                    last.then_inc(qx_ready, 1)
                if 0 <= k - 2 < STEPS:
                    norm_root(pool, link, 2, P)
                    if k - 2 >= STEPS - ROUNDS:
                        norm_root(pool, link, 2, P)
                if 0 <= k - 1 < STEPS:
                    norm_root(pool, link, 2, P)

        kg_arg, kg_trig, kg_done, k_stored = (
            sem("kg_arg"), sem("kg_trig"), sem("kg_done"), sem("k_stored"))
        TWO_PI = 6.283185307179586
        PI_PARTS = (6.28125, 0.0019350051879882812, 3.0199159819e-07)
        ROUNDER = 12582912.0
        PI_TOP = 3.1415925
        kgt = XD[:, :, :].rearrange("p k n -> p (k n)")

        def s4_col(name):
            a, w = COLS.at[name]
            return cols[:, a:a + w].rearrange("p (c n) -> p c n", c=KC)

        def kernel_act_dt(act):
            act.activation(kg[:, 0, :, 0:1], s4_col("log_dt"), ACT.Exp).then_inc(kg_trig, 1)

        def kernel_act_trig(act):
            act.wait_ge(kg_arg, 1)
            act.activation(kg[:, 3, :, :], kg[:, 1, :, :], ACT.Exp).then_inc(kg_trig, 1)
            act.activation(kg[:, 4, :, :], kg[:, 2, :, :], ACT.Sin).then_inc(kg_trig, 1)
            act.activation(kg[:, 5, :, :], kg[:, 7, :, :], ACT.Sin).then_inc(kg_trig, 1)

        def kernel_setup(pool, link):
            mul, sub, add = ALU.mult, ALU.subtract, ALU.add
            pool.wait_ge(kg_trig, 1)
            for c in range(KC):
                dt1 = kg[:, 0, c, 0:1]
                pool.tensor_scalar(kg[:, 1, c, :], s4_col("A_re")[:, c, :], dt1, None, mul)
                last = pool.tensor_scalar(kg[:, 2, c, :], s4_col("A_im")[:, c, :], dt1, None, mul)
            link(last)
            arg, n, t = kg[:, 2, :, :], kg[:, 6, :, :], kg[:, 7, :, :]
            link(pool.tensor_scalar(n, arg, 1.0 / TWO_PI, ROUNDER, mul, add))
            link(pool.tensor_scalar(n, n, -ROUNDER, None, add))
            for part in PI_PARTS:
                link(pool.tensor_scalar(t, n, part, None, mul))
                link(pool.tensor_tensor(arg, arg, t, sub))
            link(pool.tensor_scalar(arg, arg, PI_TOP, -PI_TOP, ALU.min, ALU.max))
            link(pool.tensor_scalar(t, arg, 0.0, 2.0, ALU.min, mul))
            link(pool.tensor_tensor(t, t, arg, sub))
            pool.tensor_scalar(t, t, TWO_PI / 4, None, add).then_inc(kg_arg, 1)
            pool.wait_ge(kg_trig, 4)
            zr, zi = kg[:, 1, :, :], kg[:, 2, :, :]
            pool.tensor_tensor(zr, kg[:, 3, :, :], kg[:, 5, :, :], mul)
            link(pool.tensor_tensor(zi, kg[:, 3, :, :], kg[:, 4, :, :], mul))

            def product(outs, a, b, tmp):
                pool.tensor_tensor(outs[0], a[0], b[0], mul)
                pool.tensor_tensor(tmp[0], a[1], b[1], mul)
                pool.tensor_tensor(outs[1], a[0], b[1], mul)
                link(pool.tensor_tensor(tmp[1], a[1], b[0], mul))
                pool.tensor_tensor(outs[0], outs[0], tmp[0], sub)
                link(pool.tensor_tensor(outs[1], outs[1], tmp[1], add))

            small = (kg[:, 10, :, :], kg[:, 11, :, :])
            link(pool.tensor_scalar(kg[:, 3, :, :], zr, -1.0, None, add))
            product((kg[:, 4, :, :], kg[:, 5, :, :]), (s4_col("C_re"), s4_col("C_im")), (kg[:, 3, :, :], zi), small)
            pool.tensor_tensor(kg[:, 6, :, :], s4_col("A_re"), s4_col("A_re"), mul)
            link(pool.tensor_tensor(kg[:, 7, :, :], s4_col("A_im"), s4_col("A_im"), mul))
            pool.memset(kg[:, 3, :, :], -1.0)
            link(pool.tensor_tensor(kg[:, 6, :, :], kg[:, 6, :, :], kg[:, 7, :, :], add))
            link(pool.tensor_tensor(kg[:, 6, :, :], kg[:, 6, :, :], kg[:, 3, :, :], ALU.pow))
            pool.tensor_scalar(kg[:, 8, :, :], s4_col("A_im"), -1.0, None, mul)
            link(pool.tensor_scalar(kg[:, 6, :, :], kg[:, 6, :, :], 2.0, None, mul))
            product((kg[:, 3, :, :], kg[:, 7, :, :]), (kg[:, 4, :, :], kg[:, 5, :, :]),
                    (s4_col("A_re"), kg[:, 8, :, :]), small)
            pool.tensor_tensor(kg_high[:, 0, :, 0, :], kg[:, 3, :, :], kg[:, 6, :, :], mul)
            link(pool.tensor_tensor(kg[:, 9, :, :], kg[:, 7, :, :], kg[:, 6, :, :], mul))
            pool.tensor_scalar(kg_high[:, 1, :, 0, :], kg[:, 9, :, :], -1.0, None, mul)
            pool.memset(kg_low[:, 0, :, 0, :], 1.0)
            pool.memset(kg_low[:, 1, :, 0, :], 0.0)
            pool.tensor_copy(kg_low[:, 0, :, 1, :], zr)
            link(pool.tensor_copy(kg_low[:, 1, :, 1, :], zi))
            now, then = (1, 2), (4, 5)
            m = 1
            while m < KLOW:
                product((kg[:, then[0], :, :], kg[:, then[1], :, :]), (kg[:, now[0], :, :], kg[:, now[1], :, :]),
                        (kg[:, now[0], :, :], kg[:, now[1], :, :]), small)
                now, then = then, now
                m *= 2
                if m < KLOW:
                    for c in range(KC):
                        w = m * NS
                        tmp = tuple(kgt[:, i * w:(i + 1) * w].rearrange("p (m n) -> p m n", n=NS)
                                    for i in range(2))
                        f = tuple(kg[:, j, c:c + 1, :].to_broadcast([P, m, NS]) for j in now)
                        product((kg_low[:, 0, c, m:2 * m, :], kg_low[:, 1, c, m:2 * m, :]),
                                (kg_low[:, 0, c, 0:m, :], kg_low[:, 1, c, 0:m, :]), f, tmp)
            wr, wi = kg[:, now[0], :, :], kg[:, now[1], :, :]
            for a in range(1, KHIGH):
                r0, i0 = kg_high[:, 0, :, a - 1, :], kg_high[:, 1, :, a - 1, :]
                r1, i1 = kg_high[:, 0, :, a, :], kg_high[:, 1, :, a, :]
                pool.tensor_tensor(r1, r0, wr, mul)
                pool.tensor_tensor(small[0], i0, wi, mul)
                pool.tensor_tensor(i1, i0, wr, mul)
                link(pool.tensor_tensor(small[1], r0, wi, mul))
                pool.tensor_tensor(r1, r1, small[0], add)
                link(pool.tensor_tensor(i1, i1, small[1], sub))
            link(pool.memset(k_pad[:, :, 0:T], 0.0))

        def kernel_lags(pool, link, unit):
            c, a = divmod(unit, KHIGH)
            p0 = kgt[:, 0:KLOW * NS].rearrange("p (m n) -> p m n", n=NS)
            p1 = kgt[:, KLOW * NS:2 * KLOW * NS].rearrange("p (m n) -> p m n", n=NS)
            pool.tensor_tensor(p0, kg_low[:, 0, c, :, :],
                               kg_high[:, 0, c, a:a + 1, :].to_broadcast([P, KLOW, NS]), ALU.mult)
            link(pool.tensor_tensor(p1, kg_low[:, 1, c, :, :],
                                    kg_high[:, 1, c, a:a + 1, :].to_broadcast([P, KLOW, NS]), ALU.mult))
            link(pool.tensor_tensor(p0, p0, p1, ALU.add))
            n = NS // 2
            while n > 1:
                link(pool.tensor_tensor(p0[:, :, 0:n], p0[:, :, 0:n], p0[:, :, n:2 * n], ALU.add))
                n //= 2
            dst = k_pad[:, c, T + a * KLOW:T + (a + 1) * KLOW]
            link(pool.tensor_tensor(dst.unsqueeze(2), p0[:, :, 0:1], p0[:, :, 1:2], ALU.add))

        def kernel_end(pool, link):
            k0 = k_pad[:, :, T:T + 1]
            pool.tensor_tensor(k0, k0, s4_col("D_skip"), ALU.add).then_inc(kg_done, 1)

        def kernel_store(sp):
            sp.wait_ge(kg_done, 1)
            sp.dma_start(dr["k_pad"].rearrange("(c p) m -> p c m", p=P), k_pad[:, :, :]).then_inc(k_stored, 16)

        FAR = -1e30
        e_loaded, ew1_loaded, em_loaded, e_prep = (
            sem("e_loaded"), sem("ew1_loaded"), sem("em_loaded"), sem("e_prep"))
        ectx_loaded = [sem("ectx_loaded0"), sem("ectx_loaded1")]
        t_loaded = [sem(f"t_loaded{i}") for i in range(4)]
        (m_ready, m_used, x_s_ready, x_max, x_first, x_exp, x_sel, x_rs, x_dg, fi_ready, fi_used, x2_normed, x2_affine,
         x2_ready, conv_ready, conv_copied, fo_ready, fo_used, hn_normed, hn_done, x2_b2, hf_ready, hf_copied, g_ready,
         g_done, f2x_ready, f2x_added, xa5_done) = (sem(n) for n in (
            "m_ready m_used x_s_ready x_max x_first x_exp x_sel x_rs x_dg fi_ready fi_used x2_normed x2_affine "
            "x2_ready conv_ready conv_copied fo_ready fo_used hn_normed hn_done x2_b2 hf_ready hf_copied g_ready "
            "g_done f2x_ready f2x_added xa5_done").split())
        S4_ROWS = ("g_in", "b_in", "bf_in", "bf_out", "g_ffn", "b_ffn", "b2", "g_out", "b_out")
        S4_AT = {}
        for name in S4_ROWS:
            S4_AT[name] = sum(2 * D if n[:2] == "bf" else D for n in S4_ROWS[:S4_ROWS.index(name)])

        def e_row(name, w=D):
            return e_rows[0:T, S4_AT[name]:S4_AT[name] + w]

        def e_row4(name):
            return e_row(name).unsqueeze(1).to_broadcast([T, QB, D])

        def toeplitz(j):
            k = dr["k_pad"]
            return bass.AP(tensor=k.tensor, offset=k.offset + j * TD * 2 * T + 1,
                           ap=[[1, T], [2 * T, TD], [1, T]])

        def s4x_load(sp):
            sp.wait_ge(n2_done, ROUNDS * (LAYERS - 1))
            sp.dma_start(ew, dr["e_w0"]).then_inc(e_loaded, 16)
            sp.dma_start(e_rows[:, 0:S4_AT["b_out"] + D], dr["e_rows"].partition_broadcast(P))\
                .then_inc(e_loaded, 16)
            sp.wait_ge(xa_copied, B // 2)
            sp.wait_ge(e_prep, 1)
            for h in range(XH):
                sp.dma_start(msk8[32 * h:32 * h + B, :], dr["mask2"]).then_inc(em_loaded, 16)
            sp.dma_start(tmk8[:, :], dr["mask1"])\
                .then_inc(em_loaded, 16)
            for b in range(B):
                if b >= 2:
                    sp.wait_ge(m_ready, m_count("m1", b - 2) + 1)
                for i in range(2):
                    sp.dma_start(ctx_f[0:CR[i], b % 2, i, :], dr["ctxT"][b, i * P:i * P + CR[i], :])\
                        .then_inc(ectx_loaded[b % 2], 16)
                sp.dma_start(ctx_k[:, b % 2, :, :], dr["ctx"][b].rearrange("(j p) f -> p j f", p=JR))\
                    .then_inc(ectx_loaded[b % 2], 16)
                if b == 1:
                    sp.dma_start(wc[:, 0:5250 + T], dr["e_w1"]).then_inc(ew1_loaded, 16)
                    sp.wait_ge(k_stored, 16)
                    for j in range(4):
                        sp.dma_start(t_ring[:, j, :, :], toeplitz(j)).then_inc(t_loaded[j], 16)
            for j in range(4, D // TD):
                sp.wait_ge(conv_ready, FLIPS + j - 3)
                sp.dma_start(t_ring[:, j % 4, :, :], toeplitz(j)).then_inc(t_loaded[j % 4], 16)

        def m_uses():
            uses = [("q", q) for q in range(NQ)] + [("k", 0)]
            for b in range(B):
                if b + 1 < B:
                    uses.append(("k", b + 1))
                uses += [("at", b), ("m1", b)]
                if b % QB == QB - 1:
                    uses += [("ct", 2 * (b // QB)), ("ct", 2 * (b // QB) + 1)]
            return {u: n for n, u in enumerate(uses)}

        M_AT = m_uses()

        def m_count(kind, i):
            return M_AT[(kind, i)]

        def m_claim(pe, kind, i):
            n = m_count(kind, i)
            if n >= 4:
                pe.wait_ge(m_used, n - 3)
            return ps[4 + n % 4]

        def m_bank(act, kind, i):
            n = m_count(kind, i)
            act.wait_ge(m_ready, n + 1)
            return ps[4 + n % 4]

        def s4x_pe(pe):
            pe.wait_ge(e_loaded, 32)
            pe.wait_ge(xa_copied, B // 2)
            for q in range(NQ):
                bank = m_claim(pe, "q", q)
                for k in range(KC):
                    last = pe.matmul(bank[:, 0:QT], e_wq[:, k, :], XF[:, k, q * QT:(q + 1) * QT],
                                     start=(k == 0), stop=(k == KC - 1))
                last.then_inc(m_ready, 1)

            def keys(b):
                bank = m_claim(pe, "k", b)
                pe.wait_ge(ectx_loaded[b % 2], 48 * (b // 2 + 1))
                for i in range(2):
                    last = pe.matmul(bank[:, 0:S2], e_wk[0:CR[i], i, :], ctx_f[0:CR[i], b % 2, i, :],
                                     start=(i == 0), stop=(i == 1))
                last.then_inc(m_ready, 1)

            def scores(b):
                pe.wait_ge(m_used, m_count("k", b) + 1)
                for h in range(XH):
                    n = XH * b + h
                    if n >= 4:
                        pe.wait_ge(x_exp, n - 3)
                    r = slice(32 * h, 32 * h + 32)
                    pe.matmul(ps[h][0:T, 0:S2], q_e[r, b * T:(b + 1) * T], k_e[r, b % 2, :],
                              start=True, stop=False)
                    pe.matmul(ps[h][0:T, 0:S2], ident[r, 32 * h + b:32 * h + b + 1].to_broadcast([32, T]), mskb[r, :],
                              start=False, stop=True).then_inc(x_s_ready, 1)

            def context(b):
                bank = m_claim(pe, "at", b)
                pe.wait_ge(x_dg, b + 1)
                for j in range(JC):
                    for h in range(XH):
                        last = pe.matmul(bank[0:JR, j * T:(j + 1) * T],
                                         e_p[:, XH * (b % 2) + h, j * JR:(j + 1) * JR], dg[:, b % 2, h, :],
                                         start=(h == 0), stop=(h == XH - 1))
                last.then_inc(m_ready, 1)
                bank = m_claim(pe, "m1", b)
                pe.wait_ge(m_used, m_count("at", b) + 1)
                for i in range(2):
                    for j in range(JC):
                        last = pe.matmul(bank[0:CR[i], i * T:(i + 1) * T], ctx_k[:, b % 2, j, i * P:i * P + CR[i]],
                                         at_t[:, b % 2, j, :], start=(j == 0), stop=(j == JC - 1))
                last.then_inc(m_ready, 1)

            def values(q):
                for c in range(KC):
                    bank = m_claim(pe, "ct", 2 * q + c)
                    pe.wait_ge(m_used, m_count("m1", QB * q + QB - 1) + 1)
                    for i in range(2):
                        last = pe.matmul(bank[:, 0:QT], e_wv[0:CR[i], i, c * P:(c + 1) * P],
                                         m1[0:CR[i], i, q * QT:(q + 1) * QT], start=(i == 0), stop=(i == 1))
                    last.then_inc(m_ready, 1)

            pe.wait_ge(e_prep, 3)
            keys(0)
            scores(0)
            for b in range(B):
                if b + 1 < B:
                    keys(b + 1)
                    scores(b + 1)
                context(b)
                if b % QB == QB - 1:
                    values(b // QB)
            pe.wait_ge(x_exp, B * XH)
            pe.wait_ge(m_used, len(M_AT))
            pe.wait_ge(e_prep, 5)

            def film(b, side, used, ready):
                if b >= 2:
                    pe.wait_ge(used, b - 1)
                for k in range(KC):
                    last = pe.matmul(ps[b % 2][0:T, :], c_t[:, k, b * T:(b + 1) * T], e_wf[:, side, k, :],
                                     start=(k == 0), stop=(k == KC - 1))
                last.then_inc(ready, 1)

            pe.wait_ge(ew1_loaded, 16)
            for b in range(B + 2):
                if b < B:
                    film(b, 0, fi_used, fi_ready)
                if b >= 3 and b % 2 == 1:
                    i = (b - 3) // 2
                    pe.wait_ge(x2_ready, 2 * i + 2)
                    if i >= 4:
                        pe.wait_ge(conv_copied, i - 3)
                    pe.matmul(ps[2 + i % 4][0:T, :], flip, x2[:, 2 * i:2 * i + 2, :].rearrange("t b d -> t (b d)"),
                              start=True, stop=True).then_inc(conv_ready, 1)
            pe.wait_ge(conv_copied, FLIPS)
            for j in range(D // TD):
                pe.wait_ge(t_loaded[j % 4], 16 * (j // 4 + 1))
                if j >= 4:
                    pe.wait_ge(conv_copied, FLIPS + j - 3)
                for i in range(TD):
                    last = pe.matmul(ps[2 + j % 4][0:T, i * B:(i + 1) * B], t_ring[:, j % 4, i, :],
                                     x2[:, :, j * TD + i], start=True, stop=True)
                last.then_inc(conv_ready, 1)
            pe.wait_ge(fi_used, B)
            pe.wait_ge(conv_copied, FLIPS + D // TD)

            def turn_hidden(q):
                pe.wait_ge(hn_done, 2 * (q + 1))
                if q >= 1:
                    pe.wait_ge(f2x_added, q)
                for c in range(KC):
                    for i in range(QB):
                        last = pe.transpose(ps[6 + c][:, i * T:(i + 1) * T], hn[:, i, c * P:(c + 1) * P],
                                            ident[0:T, 0:T])
                last.then_inc(hf_ready, 1)

            def feed_in(q):
                pe.wait_ge(hf_copied, q + 1)
                for m in range(8):
                    if 8 * q + m >= 4:
                        pe.wait_ge(g_done, 8 * q + m - 3)
                    for k in range(KC):
                        last = pe.matmul(ps[2 + m % 4][:, 0:QT], e_w1[:, k, m * P:(m + 1) * P], hf[:, k, :],
                                         start=(k == 0), stop=(k == KC - 1))
                    last.then_inc(g_ready, 1)

            def feed_out(q):
                pe.wait_ge(g_done, 8 * (q + 1))
                if q >= 1:
                    pe.wait_ge(xf_ready, 24 + 2 * q)
                for i in range(QB):
                    for m in range(8):
                        last = pe.matmul(ps[6 + i // 2][0:T, (i % 2) * D:(i % 2 + 1) * D],
                                         g_t[:, m, i * T:(i + 1) * T], e_w2[:, m, :],
                                         start=(m == 0), stop=(m == 7))
                last.then_inc(f2x_ready, 1)

            def turn_result(q):
                pe.wait_ge(norm_done, 12 + q + 1)
                if q + 1 < NQ:
                    pe.wait_ge(hf_copied, q + 2)
                for c in range(KC):
                    for i in range(QB):
                        last = pe.transpose(ps[6 + c][:, i * T:(i + 1) * T],
                                            XA[0:T, q * QB + i, c * P:(c + 1) * P], ident[0:T, 0:T])
                last.then_inc(xt_ready, 1)

            for i in range(QB):
                film(i, 1, fo_used, fo_ready)
            turn_hidden(0)
            for q in range(NQ):
                if q + 1 < NQ:
                    for i in range(QB):
                        film(QB * (q + 1) + i, 1, fo_used, fo_ready)
                feed_in(q)
                feed_out(q)
                if q + 1 < NQ:
                    turn_hidden(q + 1)
                turn_result(q)

        def s4x_act(act):
            act.wait_ge(xa_copied, B // 2)
            for q in range(NQ):
                act.mul(q_e[:, q * QT:(q + 1) * QT], m_bank(act, "q", q)[:, 0:QT], 32.0 ** -0.5)\
                    .then_inc(m_used, 1)

            def copy_keys(b):
                act.copy(k_e[:, b % 2, :], m_bank(act, "k", b)[:, 0:S2]).then_inc(m_used, 1)

            def copy_attention(b):
                act.copy(at_t[:, b % 2, :, :].rearrange("p j t -> p (j t)"),
                         m_bank(act, "at", b)[0:JR, 0:JC * T]).then_inc(m_used, 1)

            def copy_context(b):
                bank = m_bank(act, "m1", b)
                act.copy(m1[:, 0, b * T:(b + 1) * T], bank[:, 0:T])
                act.copy(m1[0:CR[1], 1, b * T:(b + 1) * T], bank[0:CR[1], T:2 * T]).then_inc(m_used, 1)
                if b % QB == QB - 1:
                    q = b // QB
                    for c in range(KC):
                        act.copy(c_t[:, c, q * QT:(q + 1) * QT], m_bank(act, "ct", 2 * q + c)[:, 0:QT])\
                            .then_inc(m_used, 1)

            copy_keys(0)
            copy_keys(1)
            for b in range(B):
                for h in range(XH):
                    n = XH * b + h
                    act.wait_ge(x_first, n + 1)
                    if b >= 2 and h == 0:
                        act.wait_ge(m_ready, m_count("at", b - 2) + 1)
                    act.activation(e_p[:, XH * (b % 2) + h, :], ps[h][0:T, 0:S2], ACT.Exp,
                                   bias=neg_m[:, h:h + 1]).then_inc(x_exp, 1)
                    if b >= 1 and h == 1:
                        copy_attention(b - 1)
                        copy_context(b - 1)
                        if b + 1 < B:
                            copy_keys(b + 1)
                act.wait_ge(x_rs, b + 1)
                for h in range(XH):
                    last = act.activation(dg[:, b % 2, h, :], ident[0:T, 0:T], ACT.Copy,
                                          scale=e_rs[:, b % 2, h:h + 1])
                last.then_inc(x_dg, 1)
            copy_attention(B - 1)
            copy_context(B - 1)
            for i in range(FLIPS):
                act.wait_ge(conv_ready, i + 1)
                act.copy(x2[:, 2 * i:2 * i + 2, :].rearrange("t b d -> t (b d)"), ps[2 + i % 4][0:T, :])\
                    .then_inc(conv_copied, 1)
            for j in range(D // TD):
                act.wait_ge(conv_ready, FLIPS + j + 1)
                act.copy(x2[:, :, j * TD:(j + 1) * TD].rearrange("t b d -> t d b"),
                         ps[2 + j % 4][0:T, 0:TD * B].rearrange("t (d b) -> t d b", b=B)).then_inc(conv_copied, 1)

            def copy_hidden(q):
                act.wait_ge(hf_ready, q + 1)
                act.copy(hf[:, :, :], PS[:, 6:8, 0:QT]).then_inc(hf_copied, 1)

            copy_hidden(0)
            for q in range(NQ):
                for m in range(8):
                    act.wait_ge(g_ready, 8 * q + m + 1)
                    act.activation(g_t[:, m, :], ps[2 + m % 4][:, 0:QT], ACT.Gelu,
                                   bias=col("e_b1", i=m)).then_inc(g_done, 1)
                if q + 1 < NQ:
                    copy_hidden(q + 1)
                copy_features(act, q, 6, 12 + q + 1)

        def s4x_dve(dve, link):
            dve.wait_ge(xa_copied, B // 2)
            for b in range(B):
                for h0 in range(0, XH, 2):
                    pair = [(a, h0 + a, XH * b + h0 + a) for a in range(2)]
                    cut = [0, 0]
                    for turn in range(4):
                        found = [0, 0]
                        for a, h, n in pair:
                            if turn == 0:
                                dve.wait_ge(x_s_ready, n + 1)
                            elif turn == 1:
                                dve.wait_ge(x_first, n + 1)
                            else:
                                link.after(cut[a])
                            s = ps[h][0:T, 0:S2] if turn == 0 else w_s[:, a, :]
                            found[a] = link.mark(dve.max(top8[:, a, turn, :], s))
                        if turn == 0:
                            for a, h, n in pair:
                                link.after(found[a])
                                found[a] = link.mark(dve.tensor_scalar(neg_m[:, h:h + 1], top8[:, a, 0, 0:1], -1.0,
                                                                       None, ALU.mult))
                        for a, h, n in pair:
                            link.after(found[a])
                            s = ps[h][0:T, 0:S2] if turn == 0 else w_s[:, a, :]
                            ins = dve.match_replace(w_s[:, a, :], top8[:, a, turn, :], s, FILL)
                            if turn == 0:
                                ins.then_inc(x_first, 1)
                            else:
                                cut[a] = link.mark(ins)
                    for a, h, n in pair:
                        link.after(cut[a])
                        dve.wait_ge(x_exp, n + 1)
                        e = e_p[:, XH * (b % 2) + h, :]
                        last = link.mark(dve.scalar_tensor_tensor(e, w_s[:, a, :], FILL, e, ALU.is_equal, ALU.mult,
                                                                  accum_out=e_sum[:, b % 2, h:h + 1]))
                    link.after(last)
                link(dve.reciprocal(e_rs[:, b % 2, :], e_sum[:, b % 2, :]))
                dve.tensor_scalar(e_rs[:, b % 2, :], e_rs[:, b % 2, :], tmk[:, b:b + 1], 1.0 / XH,
                                  ALU.mult, ALU.mult).then_inc(x_rs, 1)
            dve.wait_ge(m_used, len(M_AT))

            def norm_in(q):
                k = norm_stats(dve, link, [XA[0:T, q * QB + i, :] for i in range(QB)])
                for i in range(QB):
                    last = norm_apply(dve, k, i, x2[:, q * QB + i, :], XA[0:T, q * QB + i, :])
                last.then_inc(x2_normed, 1)

            def modulate(b, base, bank_ready, used, bias, more=None):
                f = film_t[:, b % 2, :]
                dve.wait_ge(bank_ready, b + 1)
                dve.tensor_tensor(f, ps[b % 2][0:T, :], e_row(bias, 2 * D), ALU.add).then_inc(used, 1)
                dve.wait_ge(used, b + 1)
                x = x2[:, b, :]
                link(dve.tensor_tensor(x, x, f[:, 0:D], ALU.mult))
                return dve.tensor_tensor(x, x, f[:, D:2 * D], ALU.add)

            norm_in(0)
            for q in range(NQ):
                if q + 1 < NQ:
                    norm_in(q + 1)
                dve.wait_ge(x2_affine, q + 1)
                for i in range(QB):
                    modulate(QB * q + i, 0, fi_ready, fi_used, "bf_in").then_inc(x2_ready, 1)
            dve.wait_ge(conv_copied, FLIPS + D // TD)

            def to_hidden(q):
                for i in range(QB):
                    b = QB * q + i
                    link(modulate(b, 0, fo_ready, fo_used, "bf_out"))
                    x = x2[:, b, :]
                    last = dve.tensor_tensor(x, x, XA[0:T, b, :], ALU.add)
                link(last)
                k = norm_stats(dve, link, [x2[:, QB * q + i, :] for i in range(QB)])
                if q >= 1:
                    dve.wait_ge(hf_ready, q)
                for i in range(QB):
                    last = norm_apply(dve, k, i, hn[:, i, :], x2[:, QB * q + i, :])
                last.then_inc(hn_done, 1)
                dve.wait_ge(hn_done, 2 * q + 1)
                link(dve.tensor_tensor(hn[:, :, :], hn[:, :, :], e_row4("g_ffn"), ALU.mult))
                dve.tensor_tensor(hn[:, :, :], hn[:, :, :], e_row4("b_ffn"), ALU.add).then_inc(hn_done, 1)

            to_hidden(0)
            for q in range(NQ):
                if q + 1 < NQ:
                    to_hidden(q + 1)
                dve.wait_ge(x2_b2, q + 1)
                dve.wait_ge(f2x_ready, q + 1)
                xs = x2[:, QB * q:QB * q + QB, :]
                dve.tensor_tensor(xs.rearrange("t (m i) d -> t m (i d)", m=2), PS[0:T, 6:8, :],
                                  xs.rearrange("t (m i) d -> t m (i d)", m=2), ALU.add).then_inc(f2x_added, 1)
                dve.wait_ge(f2x_added, q + 1)
                k = norm_stats(dve, link, [x2[:, QB * q + i, :] for i in range(QB)])
                for i in range(QB):
                    last = norm_apply(dve, k, i, x2[:, QB * q + i, :], x2[:, QB * q + i, :])
                link(last)
                link(dve.tensor_tensor(xs, xs, e_row4("g_out"), ALU.mult))
                link(dve.tensor_tensor(xs, xs, e_row4("b_out"), ALU.add))
                xa = XA[0:T, QB * q:QB * q + QB, :]
                link(dve.tensor_tensor(xa, xa, xs, ALU.add))
                norm_rows(dve, link, q)

        def s4x_pool(pool, link):
            pool.wait_ge(xa_copied, B // 2)
            pool.memset(msk8[:, :], 1).then_inc(e_prep, 1)
            pool.wait_ge(em_loaded, 16 * (XH + 1))
            pool.wait_ge(e_loaded, 32)
            pool.wait_ge(e_prep, 1)
            pool.tensor_scalar(mskb[:, :], msk8[:, :], -1.0, -FAR, ALU.add, ALU.mult).then_inc(e_prep, 1)
            pool.tensor_scalar(tmk[:, :], tmk8[:, :], 1.0, None, ALU.mult).then_inc(e_prep, 1)
            pool.tensor_scalar(e_wf, e_wf, col("gate"), None, ALU.mult).then_inc(e_prep, 1)
            for name in ("bf_in", "bf_out"):
                r = e_row(name, 2 * D)
                link(pool.tensor_scalar(r, r, col("gate", T), None, ALU.mult))
                last = pool.tensor_scalar(r[:, 0:D], r[:, 0:D], 1.0, None, ALU.add)
                link(last)
            pool.wait_ge(e_prep, 4)
            pool.memset(halves[:, :], -0.5).then_inc(e_prep, 1)
            norm_root(pool, link, QB)
            for q in range(NQ):
                x = x2[:, QB * q:QB * q + QB, :]
                pool.wait_ge(x2_normed, q + 1)
                link(pool.tensor_tensor(x, x, e_row4("g_in"), ALU.mult))
                if q + 1 < NQ:
                    norm_root(pool, link, QB)
                pool.tensor_tensor(x, x, e_row4("b_in"), ALU.add).then_inc(x2_affine, 1)
            norm_root(pool, link, QB)
            for q in range(NQ):
                x = x2[:, QB * q:QB * q + QB, :]
                pool.wait_ge(hn_done, 2 * q + 1)
                pool.tensor_tensor(x, x, e_row4("b2"), ALU.add).then_inc(x2_b2, 1)
                if q + 1 < NQ:
                    norm_root(pool, link, QB)
                norm_root(pool, link, QB)
                norm_root(pool, link, QB)

        UN = 2 * CYCLES
        (gate_dve, gn_ready, gn_done, n1_ready, n2_ready, n3_ready, tf_ready, h1_done, h2_done, h3_done,
         tf_done, cpl_done, twisted, tx_ready) = (sem(n) for n in (
             "gate_dve gn_ready gn_done n1_ready n2_ready n3_ready tf_ready h1_done h2_done h3_done "
             "tf_done cpl_done twisted tx_ready").split())

        def twi_weights():
            at, out_ = 4096, []
            for k, n in ((2, 256), (2, 128), (1, 64), (1, 1), (2, 128), (1, 64), (1, 1)):
                out_.append(wc[:, at:at + k * n].rearrange("p (k n) -> p k n", k=k))
                at += k * n
            return out_

        cn1, cn2, cn3, cn4, gc1, gc2, gc3 = twi_weights()
        BUFS = (XA, y_a, y_b, y_a)

        def twi_load(sp):
            for q in range(NQ):
                sp.wait_ge(norm_done, 16 + q + 1)
                sp.dma_start(out[q * QB:(q + 1) * QB].rearrange("b t d -> t b d"),
                             XA[0:T, q * QB:(q + 1) * QB, :]).then_inc(out_stored, 16)

        def twi_pe(pe):
            pe.wait_ge(gate_dve, 1)
            for k in range(KC):
                last = pe.matmul(ps[5][:, 0:B], gc1[:, k, :], x_sum[:, k, :], start=(k == 0), stop=(k == KC - 1))
            last.then_inc(gn_ready, 1)
            pe.wait_ge(gn_done, 1)
            pe.matmul(ps[5][0:64, B:2 * B], gc2[:, 0, :], n_g1[:, :], start=True, stop=True).then_inc(gn_ready, 1)
            pe.wait_ge(gn_done, 2)
            pe.matmul(ps[5][0:T, 2 * B:3 * B], gc3[0:64, 0, :].to_broadcast([64, T]), n_g2[:, :],
                      start=True, stop=True).then_inc(gn_ready, 1)
            pe.wait_ge(gate_dve, 2)
            for j in range(2 * UN + 4):
                if 0 <= j - 3 < 2 * UN:
                    i = j - 3
                    pe.wait_ge(h3_done, i + 1)
                    if i % 2 == 0 and i >= 2:
                        pe.wait_ge(tf_done, i // 2)
                    for b in range(QB):
                        n = (i % 2) * QB + b
                        last = pe.matmul(ps[4][0:T, n:n + 1], n_h3[:, b * T:(b + 1) * T], cn4[0:64, 0, :],
                                         start=True, stop=True)
                    last.then_inc(tf_ready, 1)
                if 0 <= j - 2 < 2 * UN:
                    pe.wait_ge(h2_done, j - 1)
                    pe.matmul(ps[3][0:64, 0:QT], cn3[:, 0, :], n_h2[:, :], start=True, stop=True)\
                        .then_inc(n3_ready, 1)
                if 0 <= j - 1 < 2 * UN:
                    pe.wait_ge(h1_done, j)
                    for k in range(KC):
                        last = pe.matmul(ps[2][:, 0:QT], cn2[:, k, :], n_h1[:, k, :], start=(k == 0),
                                         stop=(k == KC - 1))
                    last.then_inc(n2_ready, 1)
                if j >= 4 and j % 2 == 0 and j // 2 - 2 < UN - 2:
                    u = j // 2 - 2
                    pe.wait_ge(twisted, u + 1)
                    y = BUFS[u // 2 + 1]
                    for m in range(4):
                        n = 4 * u + m
                        if n >= 3:
                            pe.wait_ge(xf_ready, 32 + n - 2)
                        for i in range(QB):
                            b = (u % 2) * HB + (m // 2) * QB + i
                            last = pe.transpose(ps[5 + n % 3][:, i * T:(i + 1) * T],
                                                y[0:T, b, (m % 2) * P:(m % 2 + 1) * P], ident[0:T, 0:T])
                        last.then_inc(tx_ready, 1)
                if j < 2 * UN:
                    if j >= 4:
                        pe.wait_ge(xf_ready, 32 + 2 * (j - 3))
                    q = j % NQ
                    for m in range(KC):
                        for k in range(KC):
                            last = pe.matmul(ps[m][:, 0:QT], cn1[:, k, m * P:(m + 1) * P],
                                             XF[:, k, q * QT:(q + 1) * QT], start=(k == 0), stop=(k == KC - 1))
                    last.then_inc(n1_ready, 1)

        def twi_act(act):
            act.wait_ge(gn_ready, 1)
            act.activation(n_g1[:, :], ps[5][:, 0:B], ACT.Gelu, bias=col("gc_b1"), scale=1.0 / T)\
                .then_inc(gn_done, 1)
            act.wait_ge(gn_ready, 2)
            act.activation(n_g2[:, :], ps[5][0:64, B:2 * B], ACT.Gelu, bias=col("gc_b2", 64)).then_inc(gn_done, 1)
            act.wait_ge(gn_ready, 3)
            act.activation(cpl_0[:, :], ps[5][0:T, 2 * B:3 * B], ACT.Sigmoid, bias=col("gc_b3", T))\
                .then_inc(gn_done, 1)
            for j in range(2 * UN + 4):
                if j >= 4 and j % 2 == 0 and j // 2 - 2 < UN:
                    u = j // 2 - 2
                    act.wait_ge(tf_ready, 2 * u + 2)
                    if u >= 1:
                        act.wait_ge(cpl_done, u)
                    act.activation(tf_s[:, :], ps[4][0:T, 0:HB], ACT.Sigmoid, bias=col("cn_b4", T))\
                        .then_inc(tf_done, 1)
                if 0 <= j - 2 < 2 * UN:
                    act.wait_ge(n3_ready, j - 1)
                    act.activation(n_h3[:, :], ps[3][0:64, 0:QT], ACT.Gelu, bias=col("cn_b3", 64))\
                        .then_inc(h3_done, 1)
                if 0 <= j - 1 < 2 * UN:
                    act.wait_ge(n2_ready, j)
                    act.activation(n_h2[:, :], ps[2][:, 0:QT], ACT.Gelu, bias=col("cn_b2")).then_inc(h2_done, 1)
                if j >= 4 and j % 2 == 0 and j // 2 - 2 < UN - 2:
                    u = j // 2 - 2
                    for m in range(4):
                        n = 4 * u + m
                        q = 2 * (u % 2) + m // 2
                        act.wait_ge(tx_ready, n + 1)
                        act.copy(XF[:, m % 2, q * QT:(q + 1) * QT], ps[5 + n % 3][:, 0:QT]).then_inc(xf_ready, 1)
                if j < 2 * UN:
                    act.wait_ge(n1_ready, j + 1)
                    for m in range(KC):
                        last = act.activation(n_h1[:, m, :], ps[m][:, 0:QT], ACT.Gelu, bias=col("cn_b1", i=m))
                    last.then_inc(h1_done, 1)

        def twi_dve(dve, link):
            dve.wait_ge(xf_ready, 32)
            dve.tensor_reduce(x_sum[:, :, :], XF[:, :, :].rearrange("p k (b t) -> p k b t", t=T), AX.X, ALU.add)\
                .then_inc(gate_dve, 1)
            dve.wait_ge(gn_done, 3)
            link(dve.tensor_scalar(cpl_0[:, :], cpl_0[:, :], 0.7, -0.5, ALU.mult, ALU.add))
            link(dve.tensor_scalar(cpl_0[:, :], cpl_0[:, :], col("a_range", T), 2.0, ALU.mult, ALU.mult))
            dve.tensor_scalar(cpl_3[:, :], col("a_range", T), 0.6, None, ALU.mult)
            dve.tensor_scalar(cpl_0[:, :], cpl_0[:, :], 0.1, None, ALU.add).then_inc(gate_dve, 1)
            dve.wait_ge(gate_dve, 2)
            for u in range(UN):
                h0 = (u % 2) * HB
                old, new = BUFS[u // 2], BUFS[u // 2 + 1]
                dve.wait_ge(tf_done, u + 1)
                if u >= 1:
                    dve.wait_ge(twisted, u)
                dve.scalar_tensor_tensor(cpl[:, 0, :], tf_s[:, :], cpl_3[:, 0:1], cpl_0[:, h0:h0 + HB],
                                         ALU.mult, ALU.add).then_inc(cpl_done, 1)
                dve.wait_ge(cpl_done, u + 1)
                link(dve.tensor_scalar(cpl[:, 1, :], cpl[:, 0, :], -1.0, None, ALU.mult))
                if u // 2 == 2:
                    dve.wait_ge(tx_ready, 4 * (u - 4) + 4)
                for i in range(HB):
                    b = h0 + i
                    for dst, src, sign in ((0, 2, 0), (1, 3, 1), (2, 0, 1), (3, 1, 0)):
                        last = dve.scalar_tensor_tensor(
                            new[0:T, b, 64 * dst:64 * dst + 64], old[0:T, b, 64 * src:64 * src + 64],
                            cpl[:, sign, i:i + 1], old[0:T, b, 64 * dst:64 * dst + 64], ALU.mult, ALU.add)
                last.then_inc(twisted, 1)
                if u >= UN - 2:
                    dve.wait_ge(twisted, u + 1)
                    for q in (2 * (u % 2), 2 * (u % 2) + 1):
                        x = XA[0:T, QB * q:QB * q + QB, :]
                        link(dve.tensor_tensor(x, x, new[0:T, QB * q:QB * q + QB, :], ALU.add))
                        norm_rows(dve, link, q)

        def twi_pool(pool, link):
            for q in range(NQ):
                norm_root(pool, link, QB)

        block = ctx.enter_context(nc.Block())

        @block.sync
        def _(sp):
            ssm_load(sp)
            xat_load(sp)
            moe_small_load(sp)
            enc_first_load(sp)
            enc_load(sp)
            s4x_load(sp)
            twi_load(sp)
            sp.wait_ge(out_stored, 16 * NQ)

        @block.tensor
        def _(pe):
            ssm_pe(pe)
            xat_pe(pe)
            moe_pe(pe)
            enc_pe(pe)
            s4x_pe(pe)
            twi_pe(pe)

        @block.scalar
        def _(act):
            ssm_act(act)
            xat_act(act)
            moe_act(act)
            enc_act(act)
            s4x_act(act)
            twi_act(act)

        @block.vector
        def _(dve):
            link = Chain(dve, dve_step)
            ssm_dve(dve, link)
            xat_dve(dve, link)
            moe_dve(dve, link)
            enc_dve(dve, link)
            s4x_dve(dve, link)
            twi_dve(dve, link)

        @block.gpsimd
        def _(pool):
            link = Chain(pool, pool_step)
            ssm_pool(pool, link)
            xat_pool(pool, link)
            moe_pool(pool, link)
            enc_pool(pool, link)
            s4x_pool(pool, link)
            twi_pool(pool, link)


class _Pack:

    def __init__(self, *blocks):
        self.at, self.size = {}, 0
        for name, w in blocks:
            self.at[name] = (self.size, w)
            self.size += w


COLS = _Pack(("A_log", 32), ("b_dt", 2), ("b_xp", 1),
              ("bq", 2), ("bk", 2), ("head_mask", 2),
              ("moe_b1", 16),
              ("enc_bq", 8), ("enc_bk", 8), ("enc_b1", 32), ("diag8", 8),
              ("log_dt", 2), ("A_re", 128), ("A_im", 128), ("C_re", 128), ("C_im", 128), ("D_skip", 2),
              ("e_b1", 8), ("gate", 1),
              ("cn_b1", 2), ("cn_b2", 1), ("cn_b3", 1), ("cn_b4", 1), ("gc_b1", 1), ("gc_b2", 1), ("gc_b3", 1),
              ("a_range", 1))
ROWS = _Pack(("w_dt", D), ("b_out", D),
              ("bv", D), ("bo", D),
              ("moe_bg", 8))


def kernel(**inputs):
    import numpy as _np
    import concourse.bacc as _bacc
    from concourse.bass_utils import run_bass_kernel_spmd as _run

    a = {k: _np.asarray(v) for k, v in inputs.items()}

    def chunks(w, kc=None):
        kc = kc or -(-w.shape[0] // P)
        full = _np.zeros((kc * P, w.shape[1]), w.dtype)
        full[:w.shape[0]] = w
        return full.reshape(kc, P, -1).transpose(1, 0, 2)

    def packed(pack, values, lead):
        full = _np.zeros((lead, pack.size), _np.float32)
        for name, (at, w) in pack.at.items():
            v = values[name]
            full[:v.shape[0], at:at + w] = v
        return full

    def by_col(v):
        v = v.reshape(-1, 1)
        return chunks(v)[:, :, 0]

    cat = _np.concatenate

    def spread(w):
        full = _np.zeros((P, 4, w.shape[1]), w.dtype)
        for h in range(16):
            at = 32 * (h % 4) + 16 * (h % 2)
            full[at:at + 16, h // 4] = w[16 * h:16 * h + 16]
        return full

    L0, X0, X1 = ((lambda n, s=s: a[s + n]) for s in ("L0_attn_", "L0_xattn_", "L1_xattn_"))
    arrays = {
        "x": a["x"],
        "xT": a["x"].reshape(TOK, KC, P).transpose(1, 2, 0),
        "ident": _np.eye(P, dtype=_np.float32),
        "cols": packed(COLS, {
            "A_log": chunks(L0("A_log")).reshape(P, 32), "b_dt": by_col(L0("b_dt")),
            "b_xp": cat([by_col(L0("b_xp"))[0:32]] * 3),
            "bq": by_col(X0("bq")), "bk": by_col(X0("bk")),
            "head_mask": _np.where((_np.arange(P) // 16 % 2)[:, None] == _np.arange(2), 0.25, 0.0),
            "moe_b1": cat([by_col(v) for v in a["L0_ffn_b1"]], 1),
            "enc_bq": cat([by_col(v[0:D]) for v in a["L1_attn_bqkv"]], 1),
            "enc_bk": cat([by_col(v[D:2 * D]) for v in a["L1_attn_bqkv"]], 1),
            "enc_b1": cat([by_col(v) for v in a["L1_attn_b1"]], 1),
            "diag8": _np.where((_np.arange(P) // 16)[:, None] == _np.arange(8), 1.0, 0.0),
            **{n: chunks(X1(n)).reshape(P, -1) for n in ("A_re", "A_im", "C_re", "C_im")},
            "log_dt": by_col(X1("log_dt")), "D_skip": by_col(X1("D_skip")), "e_b1": by_col(X1("b1")),
            "gate": _np.broadcast_to(X1("mod_gate").reshape(1, 1), (P, 1)),
            **{n: by_col(a["L1_ffn_" + n]) for n in ("cn_b1", "cn_b2", "cn_b3", "gc_b1", "gc_b2")},
            **{n: _np.broadcast_to(a["L1_ffn_" + k].reshape(1, 1), (P, 1)) for n, k in (
                ("cn_b4", "cn_b4"), ("gc_b3", "gc_b3"), ("a_range", "adaptive_range"))},
        }, P),
        "rows": packed(ROWS, {
            "w_dt": L0("W_dt").reshape(1, D), "b_out": L0("b_out").reshape(1, D),
            "bv": X0("bv").reshape(1, D), "bo": X0("bo").reshape(1, D),
            "moe_bg": a["L0_ffn_b_gate"].reshape(1, 8),
        }, 1).reshape(-1),
        "wa": cat([chunks(L0("W_xp").T)] * 3 + [chunks(L0("W_out").T)], 2),
        "wo4": spread(X0("Wo").T),
        "wb": cat([chunks(X0(n).T) for n in ("Wq", "Wk", "Wv", "Wo")], 2),
        "ctxT": a["ctx_768"].transpose(0, 2, 1),
        "wc": cat([chunks(w).reshape(P, -1) for n in ("W1", "W2") for w in a["L0_ffn_" + n]], 1),
        "moe_gate": chunks(a["L0_ffn_W_gate"]).reshape(P, -1),
        "moe_b2": a["L0_ffn_b2"],
        "enc_w": _np.stack([cat([(spread if n == "Wo" else chunks)(a["L1_attn_" + n][i].T).reshape(P, -1)
                                for n in ("Wqkv", "Wo", "W1", "W2")], 1) for i in range(4)]),
        "enc_rows": _np.stack([a["L1_attn_bqkv"][:, 2 * D:]] + [
            a["L1_attn_" + n] for n in ("bo", "g1", "be1", "b2", "g2", "be2")], 1),
        "ctx": a["ctx_768"],
        "mask1": a["mask_BxS_bf1"].view(_np.uint8).T, "mask2": a["mask_BxS2_bf1"].view(_np.uint8),
        "e_w0": cat([chunks(X1(n)).reshape(P, -1) for n in ("Wq", "Wk", "Wv", "W_film_in", "W_film_out")], 1),
        "e_rows": cat([X1(n) for n in ("g_norm_in", "b_norm_in", "b_film_in", "b_film_out", "g_ffn", "b_ffn", "b2",
                                       "g_norm_out", "b_norm_out")]),
        "e_w1": cat([chunks(X1("W1")).reshape(P, -1), chunks(X1("W2")).reshape(P, -1)] + [
            chunks(a["L1_ffn_" + n]).reshape(P, -1)
            for n in ("cn_w1", "cn_w2", "cn_w3", "cn_w4", "gc_w1", "gc_w2", "gc_w3")] + [
            chunks(_np.eye(T, dtype=_np.float32)[::-1], 1)[:, 0]], 1),
    }
    nc = _bacc.Bacc("TRN2", target_bir_lowering=False, num_devices=1)
    arrays = {k: _np.ascontiguousarray(v) for k, v in arrays.items()}
    dr = {k: nc.dram_tensor(f"in_{k}", v.shape, mybir.dt.from_np(v.dtype), kind="ExternalInput").ap()
          for k, v in arrays.items()}
    dr["k_pad"] = nc.dram_tensor("k_scratch", (D, 2 * T), F32).ap()
    out = nc.dram_tensor("out_0", (B, T, D), F32, kind="ExternalOutput").ap()
    build(nc, dr, out)
    r = _run(nc, [{f"in_{k}": v for k, v in arrays.items()}], core_ids=[0])
    return r.results[0]["out_0"]
```
